# Optimizing a Trainium2 kernel written in Bass

```python
import numpy as np
import jax
import jax.numpy as jnp

def _softmax(x, axis=-1):
    return jax.nn.softmax(x, axis=axis)

def _gelu(x):
    return jax.nn.gelu(x, approximate=True)

def _silu(x):
    return jax.nn.silu(x)

def _sigmoid(x):
    return jax.nn.sigmoid(x)

def _layernorm(x, axis=-1, eps=1e-05):
    m = jnp.mean(x, axis=axis, keepdims=True)
    v = jnp.var(x, axis=axis, keepdims=True)
    return (x - m) / jnp.sqrt(v + eps)

def _scatter_add(tgt, idx, src, axis=0):
    return tgt.at[idx].add(src)

def _segment_sum(src, seg, n):
    return jax.ops.segment_sum(src, seg, n)
kernel_name = 'mk_adaln_ffn_d1_seqx_r4_78fc6b'

def setup_inputs(seed: int=0):
    np.random.seed(seed)
    _w = jnp.asarray

    def _rec_inputs():
        import jax
        import jax.numpy as jnp
        _rk = jax.random.key(seed)
        x = 7.22e-05 + 1 * jax.random.normal(jax.random.fold_in(_rk, 1), (32, 256, 256), jnp.float32)
        _lenS = 256 - jax.random.randint(jax.random.fold_in(_rk, 7), (32,), 0, max(1, 256 // 4) + 1, jnp.int32)
        _lenS2 = 256 - jax.random.randint(jax.random.fold_in(_rk, 8), (32,), 0, max(1, 256 // 4) + 1, jnp.int32)
        cond_512 = 0.0061147 + 1.02565 * jax.random.normal(jax.random.fold_in(_rk, 11), (32, 128), jnp.float32)
        return (x, cond_512)
    x, cond_512 = _rec_inputs()

    def _L0_cond_setup():
        import jax, jax.numpy as jnp
        import numpy as np
        import math
        HEAD_NUM = 16
        EPS = 1e-08

        def modulated_linear(x, s, aff_w, aff_b, w, b):
            style = s @ aff_w.T + aff_b
            w_mod = w[None, :, :] * style[:, None, :]
            demod = jax.lax.rsqrt(jnp.sum(w_mod * w_mod, axis=2) + EPS)
            w_mod = w_mod * demod[:, :, None]
            return jnp.einsum('bni,boi->bno', x, w_mod) + b
        key = jax.random.key(seed)
        ks = jax.random.split(key, 6)
        B, N, F, S = (8, 256, 256, 128)
        return {'x': jax.random.normal(ks[0], (B, N, F), dtype=jnp.float32), 's': jax.random.normal(ks[1], (B, S), dtype=jnp.float32), 'k_aff_w': jax.random.normal(ks[2], (F, S), dtype=jnp.float32) * 0.02, 'k_aff_b': jnp.ones((F,), dtype=jnp.float32), 'k_w': jax.random.normal(ks[3], (F, F), dtype=jnp.float32) * 0.02, 'k_b': jnp.zeros((F,), dtype=jnp.float32), 'o_aff_w': jax.random.normal(ks[4], (F, S), dtype=jnp.float32) * 0.02, 'o_aff_b': jnp.ones((F,), dtype=jnp.float32), 'o_w': jax.random.normal(ks[5], (F, F), dtype=jnp.float32) * 0.02, 'o_b': jnp.zeros((F,), dtype=jnp.float32)}
    _L0_cond_all = _L0_cond_setup()
    _L0_cond_in = {k: v for k, v in _L0_cond_all.items() if k in ('k_aff_w', 'k_aff_b', 'k_w', 'k_b', 'o_aff_w', 'o_aff_b', 'o_w', 'o_b')}
    del _L0_cond_all

    def _L0_ffn_setup():
        import jax, jax.numpy as jnp
        import numpy as np
        B, S, H = (2, 512, 256)
        N, F, SF, K = (16, 256, 1024, 1)
        key = jax.random.key(seed)
        ks = jax.random.split(key, 7)
        std = 0.02
        return {'hidden_states': jax.random.normal(ks[0], (B, S, H), dtype=jnp.float32), 'router_w': jax.random.normal(ks[1], (N, H), dtype=jnp.float32) * std, 'gate_up_proj': jax.random.normal(ks[2], (N, H, 2 * F), dtype=jnp.float32) * std, 'down_proj': jax.random.normal(ks[3], (N, F, H), dtype=jnp.float32) * std, 'shared_gate_w': jax.random.normal(ks[4], (SF, H), dtype=jnp.float32) * std, 'shared_up_w': jax.random.normal(ks[5], (SF, H), dtype=jnp.float32) * std, 'shared_down_w': jax.random.normal(ks[6], (H, SF), dtype=jnp.float32) * std}
    _L0_ffn_all = _L0_ffn_setup()
    _L0_ffn_in = {k: v for k, v in _L0_ffn_all.items() if k in ('router_w', 'gate_up_proj', 'down_proj', 'shared_gate_w', 'shared_up_w', 'shared_down_w')}
    del _L0_ffn_all
    return {'x': x, 'cond_512': cond_512, 'L0_cond_k_aff_w': _L0_cond_in['k_aff_w'], 'L0_cond_k_aff_b': _L0_cond_in['k_aff_b'], 'L0_cond_k_w': _L0_cond_in['k_w'], 'L0_cond_k_b': _L0_cond_in['k_b'], 'L0_cond_o_aff_w': _L0_cond_in['o_aff_w'], 'L0_cond_o_aff_b': _L0_cond_in['o_aff_b'], 'L0_cond_o_w': _L0_cond_in['o_w'], 'L0_cond_o_b': _L0_cond_in['o_b'], 'L0_ffn_router_w': _L0_ffn_in['router_w'], 'L0_ffn_gate_up_proj': _L0_ffn_in['gate_up_proj'], 'L0_ffn_down_proj': _L0_ffn_in['down_proj'], 'L0_ffn_shared_gate_w': _L0_ffn_in['shared_gate_w'], 'L0_ffn_shared_up_w': _L0_ffn_in['shared_up_w'], 'L0_ffn_shared_down_w': _L0_ffn_in['shared_down_w']}

def reference(x, cond_512, L0_cond_k_aff_w, L0_cond_k_aff_b, L0_cond_k_w, L0_cond_k_b, L0_cond_o_aff_w, L0_cond_o_aff_b, L0_cond_o_w, L0_cond_o_b, L0_ffn_router_w, L0_ffn_gate_up_proj, L0_ffn_down_proj, L0_ffn_shared_gate_w, L0_ffn_shared_up_w, L0_ffn_shared_down_w):
    import jax
    import jax.numpy as jnp

    def _L0_cond_ref(x, s, k_aff_w, k_aff_b, k_w, k_b, o_aff_w, o_aff_b, o_w, o_b):
        import jax, jax.numpy as jnp
        import numpy as np
        import math
        HEAD_NUM = 16
        EPS = 1e-08

        def modulated_linear(x, s, aff_w, aff_b, w, b):
            style = s @ aff_w.T + aff_b
            w_mod = w[None, :, :] * style[:, None, :]
            demod = jax.lax.rsqrt(jnp.sum(w_mod * w_mod, axis=2) + EPS)
            w_mod = w_mod * demod[:, :, None]
            return jnp.einsum('bni,boi->bno', x, w_mod) + b
        B, N, F = x.shape
        H = HEAD_NUM
        D = F // H
        kx = modulated_linear(x, s, k_aff_w, k_aff_b, k_w, k_b)
        kx = kx.reshape(B, N, H, D)
        q = k = v = kx
        scores = jnp.einsum('bnhd,bnjd->bnhj', q, k) / math.sqrt(D)
        A = jax.nn.softmax(scores, axis=-1)
        out = jnp.einsum('bnhj,bnjd->bnhd', A, v).reshape(B, N, F)
        out = modulated_linear(out, s, o_aff_w, o_aff_b, o_w, o_b)
        return out

    def _L0_ffn_ref(hidden_states, router_w, gate_up_proj, down_proj, shared_gate_w, shared_up_w, shared_down_w):
        import jax, jax.numpy as jnp
        import numpy as np
        B, S, H = (2, 512, 256)
        N, F, SF, K = (16, 256, 1024, 1)
        b, s, h = hidden_states.shape
        hidden = hidden_states.reshape(-1, h)
        t = hidden.shape[0]
        logits = hidden @ router_w.T
        top_vals, top_idx = jax.lax.top_k(logits, K)
        scores = jnp.full_like(logits, -jnp.inf)
        scores = scores.at[jnp.arange(t)[:, None], top_idx].set(top_vals)
        scores = jax.nn.sigmoid(scores.astype(jnp.float32)).astype(hidden.dtype)
        routed_in = hidden[None, :, :] * scores.T[:, :, None]
        gate_up = jnp.einsum('nth,nhf->ntf', routed_in, gate_up_proj)
        gate, up = jnp.split(gate_up, 2, axis=-1)
        routed_out = jnp.einsum('ntf,nfh->nth', up * jax.nn.silu(gate), down_proj)
        expert_sum = routed_out.sum(axis=0)
        shared = jax.nn.silu(hidden @ shared_gate_w.T) * (hidden @ shared_up_w.T) @ shared_down_w.T
        return (shared + expert_sum).reshape(b, s, h)
    x = x + _L0_ffn_ref(_L0_cond_ref(x, cond_512, L0_cond_k_aff_w, L0_cond_k_aff_b, L0_cond_k_w, L0_cond_k_b, L0_cond_o_aff_w, L0_cond_o_aff_b, L0_cond_o_w, L0_cond_o_b), L0_ffn_router_w, L0_ffn_gate_up_proj, L0_ffn_down_proj, L0_ffn_shared_gate_w, L0_ffn_shared_up_w, L0_ffn_shared_down_w)
    return x

_drawn_inputs = setup_inputs


def setup_inputs(seed=0):
    import zlib

    import numpy as np

    out = dict(_drawn_inputs(seed))
    spreads = {'L0_cond_k_aff_b': (1.0, 0.6),
     'L0_cond_k_b': (0.0, 0.8),
     'L0_cond_o_aff_b': (1.0, 0.6),
     'L0_cond_o_b': (0.0, 0.8)}
    factors = {'cond_512': 5.259,
     'L0_cond_k_aff_w': 6.933,
     'L0_cond_o_aff_w': 7.462,
     'L0_ffn_router_w': 8.0,
     'L0_ffn_gate_up_proj': 8.0,
     'L0_ffn_down_proj': 8.0,
     'L0_ffn_shared_gate_w': 8.0,
     'L0_ffn_shared_up_w': 8.0,
     'L0_ffn_shared_down_w': 8.0}
    for name, (base, spread) in spreads.items():
        noise = np.random.default_rng([zlib.crc32(name.encode()), seed]).standard_normal(out[name].shape)
        drawn = base * np.exp(spread * noise) if base else spread * noise
        out[name] = jnp.asarray(drawn.astype(out[name].dtype))
    for name, factor in factors.items():
        out[name] = (out[name] * factor).astype(out[name].dtype)
    return out
```

```python
from contextlib import ExitStack

import concourse.bass as bass
from concourse import mybir

F32 = mybir.dt.float32
BF16 = mybir.dt.bfloat16
I32 = mybir.dt.int32
ALU = mybir.AluOpType
ACT = mybir.ActivationFunctionType
AX = mybir.AxisListType

P = 128
BATCH, SEQ, F = 32, 256, 256
COND = 128
HEADS, D = 16, 16
EXPERTS, EF = 16, 256
SF = 1024
TOKENS = BATCH * SEQ
KT = F // P
CHUNK = 512
TILES = CHUNK // P
CB = CHUNK // SEQ
NCHUNK = TOKENS // CHUNK
Q = 4
PAIRS = 16
JT = SF // P
NMOD = 6
ROUTED = TOKENS // P + EXPERTS
LEAD = 7
UNROLL = 10
TABLE = EXPERTS * TOKENS + ROUTED * P
EMPTY = TOKENS
EPS = 1e-8
MASKED = -1e30
SCALE = 1.0 / D ** 0.5

C_ID = 0
C_TRI = C_ID + P
C_ML = C_TRI + P
C_MR = C_ML + P
C_REV = C_MR + PAIRS * 32
C_BASE = C_REV + EXPERTS
C_STEP = C_BASE + EXPERTS
C_TILE = C_STEP + TOKENS // P
C_TOK = C_TILE + ROUTED
C_END = C_TOK + TILES
ARENA = UNROLL * 2 * F + 8 * F + UNROLL * F


def build_program(nc, xT, x, condT, k_affT, k_wT, k_b, o_affT, o_wT, bias_cols, routerT,
                  gate_up, down, sh_gateT, sh_upT, sh_downT, consts, out):
    demod_rows = nc.dram_tensor("demod_rows", [BATCH, F], F32).ap()
    slot_table = nc.dram_tensor("slot_table", [TABLE, 1], I32).ap()
    rows = nc.dram_tensor("routed_rows", [TOKENS + 1, 2 * F], F32).ap()

    ctx = ExitStack()
    with ctx:
        def sb(name, shape, dt=F32):
            return ctx.enter_context(nc.sbuf_tensor("sb_" + name, shape, dt))

        made = {}
        passed = {nc.sync: "loads_passed", nc.gpsimd: "indirect_passed"}

        def sem(name):
            if name not in made:
                made[name] = ctx.enter_context(nc.semaphore(name))
            return made[name]

        def wait(eng, name, n):
            if not isinstance(n, int) or n > 0:
                eng.wait_ge(sem(name), n)
            if not isinstance(n, int) and eng in passed:
                eng.sem_inc(sem(passed[eng]), 1)

        cst = sb("consts", [P, C_END])
        tri = sb("tri", [P, P], BF16)
        ones = sb("ones", [P, P], BF16)
        mask_l = sb("mask_l", [2, P], BF16)
        mask_r = sb("mask_r", [2, PAIRS * 32], BF16)
        wk = sb("wk", [P, KT, F])
        wo = sb("wo", [P, KT, F])
        w_router = sb("w_router", [P, KT, EXPERTS])
        w_gate = sb("w_gate", [P, KT, SF])
        w_up = sb("w_up", [P, KT, SF])
        w_down = sb("w_down", [P, JT, F])
        e_gu = sb("e_gu", [P, EXPERTS, KT, 2 * EF])
        e_down = sb("e_down", [P, EXPERTS, KT, F])
        bias_k = sb("bias_k", [P, F])
        biases = sb("biases", [P, 3 * KT])
        mods = sb("mods", [P, NCHUNK, NMOD, CB])
        mod = sb("mod", [P, NMOD, CB])
        arena = sb("arena", [P, ARENA])
        taken = [0]

        def part(*shape):
            n = 1
            for m in shape:
                n *= m
            lo = taken[0]
            taken[0] += n
            ap = arena[:, lo:lo + n]
            names = "abc"[:len(shape)]
            if len(shape) > 1:
                ap = ap.rearrange(f"p ({' '.join(names)}) -> p {' '.join(names)}", **dict(zip(names[1:], shape[1:])))
            return ap

        xt = part(KT, CHUNK)
        wkb = part(CB, KT, F)
        kpad = part(HEADS, 2, D)
        keyT = part(2, 32 * HEADS)
        val = part(2, PAIRS * 32)
        sc = part(PAIRS, 32)
        probT = part(2, PAIRS * 32)
        ot = part(HEADS, 2, D)
        att = part(HEADS * D)
        aT = part(KT, CHUNK)
        demod_b = sb("demod_b", [P, CB, F])
        rowmax = sb("rowmax", [P, PAIRS])
        rz = sb("rz", [P, HEADS])
        yT = sb("yT", [P, KT, CHUNK])
        xr = sb("xr", [P, TILES, F])
        silu = sb("silu", [P, 2, CHUNK])
        hid = sb("hid", [P, 2, CHUNK])
        base = sb("base", [P, TILES, F])
        ys = sb("ys", [P, TILES, F])
        top = sb("top", [P, TILES])
        expt = sb("expt", [P, TILES])
        ex1 = sb("ex1", [P, TILES])
        score = sb("score", [P, TILES])
        eq = sb("eq", [P, TILES, EXPERTS])
        pick = sb("pick", [P, TILES, EXPERTS])
        pickmax = sb("pickmax", [P, TILES])
        onehot = sb("onehot", [P, TILES, EXPERTS], BF16)
        rank = sb("rank", [P, TILES, EXPERTS])
        slotsel = sb("slotsel", [P, TILES, EXPERTS])
        slotf = sb("slotf", [P, TILES])
        slot = sb("slot", [P, TILES], I32)
        tokid = sb("tokid", [P, TILES], I32)
        count = sb("count", [P, EXPERTS])
        held = sb("held", [1, EXPERTS])
        ntile = sb("ntile", [1, EXPERTS])
        tend = sb("tend", [1, EXPERTS])
        which = sb("which", [1, ROUTED])
        first = sb("first", [1, ROUTED])
        within = sb("within", [1, ROUTED])
        offf = sb("offf", [1, ROUTED])
        wofff = sb("wofff", [1, ROUTED])
        off = sb("off", [1, ROUTED], I32)
        woff = sb("woff", [1, ROUTED], I32)
        idx = sb("idx", [P, UNROLL], I32)
        taken[0] = 0
        gat = part(UNROLL, 2 * F)
        rxT = part(2, KT * P)
        rsilu = part(2, EF)
        rhid = part(2, EF)
        rhT = part(2, KT * P)
        res = part(UNROLL, F)
        taken[0] = 0
        more = part(EXPERTS, TOKENS // P)[0:1]
        before = part(ROUTED, EXPERTS)[0:1]
        weighed = part(ROUTED, EXPERTS)[0:1]

        bank = [ctx.enter_context(nc.psum_tensor(f"bank{i}", [P, 512], F32)) for i in range(8)]
        ps_gate, ps_up, ps_sh0, ps_sh1, ps_k, ps_s, ps_o, ps_t = bank
        ident = cst[:, C_ID:C_ID + P]
        erev = cst[:, C_REV:C_REV + EXPERTS]

        def modview(w0, w1):
            return mods[:, :, w0:w1, :]

        block = ctx.enter_context(nc.Block())

        @block.sync
        def _(sp):
            sp.dma_start(cst[:, :], consts).then_inc(sem("consts_in"), 16)
            sp.dma_start(ot[:, 0:HEADS, :, :].rearrange("p h s d -> p (h s d)")[:, 0:BATCH], condT)\
                .then_inc(sem("cond_in"), 16)
            sp.dma_start(att[:, 0:F], k_affT).then_inc(sem("cond_in"), 16)
            sp.dma_start(sc[:, :, :].rearrange("p a b -> p (a b)")[:, 0:F], o_affT).then_inc(sem("cond_in"), 16)
            sp.dma_start(wk[:, :, :], k_wT.rearrange("(k p) o -> p k o", p=P)).then_inc(sem("wk_in"), 16)
            sp.dma_start(wo[:, :, :], o_wT.rearrange("(k p) o -> p k o", p=P)).then_inc(sem("wk_in"), 16)
            sp.dma_start(biases[:, :], bias_cols).then_inc(sem("bias_in"), 16)
            sp.dma_start(bias_k[:, :], k_b.partition_broadcast(P)).then_inc(sem("bias_in"), 16)
            sp.dma_start(xt[:, :, :], xT[0, :, :, :]).then_inc(sem("xt_in"), 16)
            sp.dma_start(w_gate[:, :, :], sh_gateT.rearrange("(k p) o -> p k o", p=P)).then_inc(sem("shared_in"), 16)
            sp.dma_start(w_up[:, :, :], sh_upT.rearrange("(k p) o -> p k o", p=P)).then_inc(sem("shared_in"), 16)
            sp.dma_start(w_down[:, :, :], sh_downT.rearrange("(j p) o -> p j o", p=P)).then_inc(sem("shared_in"), 16)
            sp.dma_start(w_router[:, :, :], routerT.rearrange("(k p) o -> p k o", p=P)).then_inc(sem("shared_in"), 16)
            sp.wait_ge(sem("fill_ready"), 2)
            fill = ys[:, :, :].rearrange("p t f -> p (t f)").bitcast(I32)
            whole = EXPERTS * TOKENS
            sp.dma_start(slot_table[0:whole, :].rearrange("(p t) o -> p (t o)", p=P), fill)\
                .then_inc(sem("filled"), 16)
            sp.dma_start(slot_table[whole:TABLE, :].rearrange("(p t) o -> p (t o)", p=P), fill[:, 0:ROUTED])\
                .then_inc(sem("filled"), 16)
            sp.dma_start(rows[TOKENS:TOKENS + 1, :], base[0:1, 0:2, :].rearrange("p t f -> p (t f)"))\
                .then_inc(sem("filled"), 16)
            sp.wait_ge(sem("demod_k"), 1)
            sp.dma_start(demod_rows, sc[0:BATCH, :, :].rearrange("p a b -> p (a b)")[:, F:2 * F])\
                .then_inc(sem("demod_out"), 16)
            sp.wait_ge(sem("demod_out"), 16)
            sp.dma_start(demod_b[:, :, :], demod_rows[0:CB, :].partition_broadcast(P)).then_inc(sem("demod_in"), 16)

            def chunk(it, att_on, ffn_on, ahead):
                if ffn_on:
                    wait(sp, "base_ready", it - 1)
                    sp.dma_start(xr[:, :, :], x[bass.ds((it - 1) * TILES, TILES), :, :].rearrange("t p f -> p t f"))\
                        .then_inc(sem("xr_in"), 16)
                if ahead:
                    wait(sp, "wkb_ready", it + 1)
                    sp.dma_start(demod_b[:, :, :],
                                 demod_rows[bass.ds((it + 1) * CB, CB), :].partition_broadcast(P))\
                        .then_inc(sem("demod_in"), 16)
                if ffn_on:
                    wait(sp, "ys_ready", TILES * it)
                    sp.dma_start(rows[bass.ds((it - 1) * CHUNK, CHUNK), 0:F].rearrange("(t p) f -> p t f", p=P),
                                 ys[:, :, :]).then_inc(sem("ys_out"), 16)
                if ahead:
                    wait(sp, "proj_done", TILES * (it + 1))
                    sp.dma_start(xt[:, :, :], xT[bass.ds(it + 1, 1), :, :, :].rearrange("a p k t -> p (a k) t"))\
                        .then_inc(sem("xt_in"), 16)
                if att_on:
                    sp.dma_start(e_gu[:, bass.ds(it, 1), :, :].rearrange("p e k f -> p (e k) f"),
                                 gate_up[bass.ds(it, 1), :, :].rearrange("e (k p) f -> p (e k) f", p=P))\
                        .then_inc(sem("expert_in"), 16)
                    sp.dma_start(e_down[:, bass.ds(it, 1), :, :].rearrange("p e k f -> p (e k) f"),
                                 down[bass.ds(it, 1), :, :].rearrange("e (k p) f -> p (e k) f", p=P))\
                        .then_inc(sem("expert_in"), 16)
                if ffn_on:
                    wait(sp, "base_ready", it)
                    sp.dma_start(rows[bass.ds((it - 1) * CHUNK, CHUNK), F:2 * F].rearrange("(t p) f -> p t f", p=P),
                                 base[:, :, :]).then_inc(sem("base_out"), 16)

            chunk(0, True, False, True)
            chunk(1, True, True, True)
            with sp.Fori(2, NCHUNK - 1) as it:
                chunk(it, True, True, True)
            chunk(NCHUNK - 1, True, True, False)
            chunk(NCHUNK, False, True, False)
            sp.wait_ge(sem("slots_out"), 16 * TILES * NCHUNK)
            sp.wait_ge(sem("list_ready"), 2)
            with sp.Fori(0, ROUTED // UNROLL) as g:
                for u in range(UNROLL):
                    at = sp.value_load(off[0:1, bass.ds(UNROLL * g + u, 1)], min_val=0, max_val=TABLE - P)
                    wait(sp, f"res_out{u}", 16 * g)
                    sp.dma_start(idx[:, u:u + 1], slot_table[bass.ds(at, P), :]).then_inc(sem(f"idx_in{u}"), 16)

        @block.gpsimd
        def _(pool):
            pool.memset(ys[:, :, :].rearrange("p t f -> p (t f)").bitcast(I32), EMPTY).then_inc(sem("fill_ready"), 1)
            pool.memset(base[0:1, 0:2, :], 0.0).then_inc(sem("fill_ready"), 1)
            pool.memset(ones[:, :], 1.0).then_inc(sem("ones_ready"), 1)

            def scatter_ids(f):
                wait(pool, "slot_ready", f + 1)
                for t in range(TILES):
                    pool.indirect_dma_start(slot_table[:, :], bass.IndirectOffsetOnAxis(slot[:, t:t + 1], 0),
                                            tokid[:, t:t + 1], None, bounds_check=TABLE - 1, oob_is_err=False)\
                        .then_inc(sem("slots_out"), 16)

            with pool.Fori(0, NCHUNK) as f:
                scatter_ids(f)

            pool.wait_ge(sem("ys_out"), 16 * NCHUNK)
            pool.wait_ge(sem("base_out"), 16 * NCHUNK)

            def gather(g, u):
                wait(pool, f"idx_in{u}", 16 * (g + 1))
                pool.indirect_dma_start(gat[:, u, :], None, rows[:, :],
                                        bass.IndirectOffsetOnAxis(idx[:, u:u + 1], 0), bounds_check=TOKENS, oob_is_err=False)\
                    .then_inc(sem(f"gat_in{u}"), 16)

            def scatter(g, u):
                wait(pool, "res_ready", g * UNROLL + u + 1)
                pool.indirect_dma_start(out, bass.IndirectOffsetOnAxis(idx[:, u:u + 1], 0),
                                        res[:, u, :], None, bounds_check=TOKENS - 1, oob_is_err=False)\
                    .then_inc(sem(f"res_out{u}"), 16)

            last = ROUTED // UNROLL - 1

            def step(g, u, last_body):
                if not (last_body and u + LEAD >= UNROLL):
                    gather(g + (u + LEAD) // UNROLL, (u + LEAD) % UNROLL)
                scatter(g, u)

            pool.wait_ge(sem("filled"), 48)
            for u in range(LEAD):
                gather(0, u)
            for u in range(UNROLL):
                step(0, u, False)
            with pool.Fori(1, last) as g:
                for u in range(UNROLL):
                    step(g, u, False)
            for u in range(UNROLL):
                step(last, u, True)
            for u in range(UNROLL):
                pool.wait_ge(sem(f"res_out{u}"), 16 * (last + 1))

        @block.tensor
        def _(pe):
            mm = nc.tensor.matmul
            cond = ot[:, :, :, :].rearrange("p h s d -> p (h s d)")[:, 0:BATCH]
            affo = sc[:, :, :].rearrange("p a b -> p (a b)")[:, 0:F]
            pe.wait_ge(sem("cond_in"), 48)
            for w in range(2 * KT):
                src = att[:, (w % KT) * P:(w % KT + 1) * P] if w < KT else affo[:, (w % KT) * P:(w % KT + 1) * P]
                last = mm(ps_k[:, w * BATCH:(w + 1) * BATCH], src, cond, start=True, stop=True)
            last.then_inc(sem("style_done"), 1)
            pe.wait_ge(sem("squares_ready"), 2)
            sq = kpad[:, :, :, :].rearrange("p h s d -> p (h s d)")
            w2 = keyT[:, :, :]
            for k in range(KT):
                last = mm(ps_s[0:BATCH, 0:F], sq[:, k * BATCH:(k + 1) * BATCH], w2[:, 0, k * F:(k + 1) * F],
                          start=(k == 0), stop=(k == KT - 1))
            last.then_inc(sem("sumsq_done"), 1)
            for o in range(KT):
                for k in range(KT):
                    last = mm(ps_o[:, o * BATCH:(o + 1) * BATCH], w2[:, 1, k * F + o * P:k * F + (o + 1) * P],
                              sq[:, (KT + k) * BATCH:(KT + k + 1) * BATCH], start=(k == 0), stop=(k == KT - 1))
            last.then_inc(sem("sumsq_done"), 1)

            def project(it, t):
                wait(pe, "wkb_ready", it + 1)
                if t == 0:
                    wait(pe, "xt_in", 16 * (it + 1))
                    wait(pe, "yT_ready", KT * CB * it)
                wait(pe, "k_taken", TILES * it + t)
                for k in range(KT):
                    last = mm(ps_k[:, 0:F], xt[:, k, t * P:(t + 1) * P], wkb[:, t // (TILES // CB), k, :],
                              start=(k == 0), stop=(k == KT - 1))
                last.then_inc(sem("proj_done"), 1)

            def gram(it, t, ffn_on):
                wait(pe, "keyT_ready", TILES * it + t + 1)
                wait(pe, "s_taken", TILES * it + t)
                if t == 0 and ffn_on:
                    wait(pe, "ys_ready", TILES * it)
                pe.wait_ge(sem("masks_ready"), 4)
                mm(ps_s[:, :], mask_l[:, :], mask_r[:, :], start=True, stop=False, skip_group_check=True)
                for pr in range(PAIRS):
                    for q in range(Q):
                        keys = keyT[32 * q:32 * q + D, t % 2, 32 * pr:32 * pr + 32]
                        last = mm(ps_s[32 * q:32 * q + 32, 32 * pr:32 * pr + 32], keys, keys, start=False,
                                  stop=(pr == PAIRS - 1), tile_position=(32 * q, 32 * q), skip_group_check=True)
                last.then_inc(sem("gram_done"), 1)

            def attend(it, t):
                pe.wait_ge(sem("masks_ready"), 4)
                wait(pe, "probT_ready", TILES * it + t + 1)
                wait(pe, "o_taken", TILES * it + t)
                for pr in range(PAIRS):
                    for q in range(Q):
                        last = mm(ps_o[32 * q:32 * q + 32, 32 * pr:32 * pr + 32],
                                  val[32 * q:32 * q + 32, t % 2, 32 * pr:32 * pr + 32],
                                  probT[32 * q:32 * q + 32, t % 2, 32 * pr:32 * pr + 32],
                                  start=True, stop=True, tile_position=(32 * q, 32 * q), skip_group_check=True)
                last.then_inc(sem("av_done"), 1)

            def turn(it, t):
                wait(pe, "att_ready", TILES * it + t + 1)
                if t == 0:
                    wait(pe, "rank_taken", it)
                    wait(pe, "yT_ready", KT * CB * it)
                wait(pe, "aT_ready", TILES * it + t)
                for k in range(KT):
                    last = nc.tensor.transpose(ps_t[:, k * P:(k + 1) * P], att[:, k * P:(k + 1) * P], ident)
                last.then_inc(sem("turn_done"), 1)

            def out_linear(it):
                wait(pe, "aT_ready", TILES * (it + 1))
                for o in range(KT):
                    bk = (ps_k, ps_t)[o]
                    for k in range(KT):
                        last = mm(bk[:, :], wo[:, k, o * P:(o + 1) * P], aT[:, k, :], start=(k == 0),
                                  stop=(k == KT - 1))
                    last.then_inc(sem("y_done"), 1)

            def shared_in(f, j):
                if j == 0:
                    wait(pe, "yT_ready", KT * CB * (f + 1))
                wait(pe, "silu_ready", JT * f + j)
                for wgt, bk, name in ((w_gate, ps_gate, "gate_done"), (w_up, ps_up, "up_done")):
                    if wgt is w_up:
                        wait(pe, "hid_ready", JT * f + j)
                    for k in range(KT):
                        last = mm(bk[:, :], wgt[:, k, j * P:(j + 1) * P], yT[:, k, :], start=(k == 0),
                                  stop=(k == KT - 1))
                    last.then_inc(sem(name), 1)

            def shared_out(f, j):
                wait(pe, "hid_ready", JT * f + j + 1)
                if j == 0:
                    wait(pe, "base_ready", f)
                for t in range(TILES):
                    bk = (ps_sh0, ps_sh1)[t // 2]
                    last = mm(bk[:, (t % 2) * F:(t % 2 + 1) * F], hid[:, j % 2, t * P:(t + 1) * P],
                              w_down[:, j, :], start=(j == 0 and t % 2 == 0), stop=(j == JT - 1),
                              skip_group_check=True)
                last.then_inc(sem("down_done"), 1)

            def route_in(f):
                wait(pe, "aT_ready", TILES * (f + 1))
                for t in range(TILES):
                    for k in range(KT):
                        last = mm(ps_t[:, t * EXPERTS:(t + 1) * EXPERTS], yT[:, k, t * P:(t + 1) * P],
                                  w_router[:, k, :], start=(k == 0), stop=(k == KT - 1), skip_group_check=True)
                last.then_inc(sem("logit_done"), 1)
                wait(pe, "s_taken", TILES * (f + 1))
                wait(pe, "o_taken", TILES * (f + 1))
                for t in range(TILES):
                    bk = (ps_s, ps_o)[t // 2]
                    for k in range(KT):
                        last = nc.tensor.transpose(bk[:, (t % 2) * F + k * P:(t % 2) * F + (k + 1) * P],
                                                   yT[:, k, t * P:(t + 1) * P], ident)
                    last.then_inc(sem("yrow_done"), 1)

            def route_rank(f):
                wait(pe, "onehot_ready", f + 1)
                width = TILES * EXPERTS
                oh = onehot[:, :, :].rearrange("p t e -> p (t e)")
                mm(ps_t[:, 0:width], tri[:, :], oh, start=True, stop=False, skip_group_check=True)
                for t in range(TILES - 1):
                    lo = (t + 1) * EXPERTS
                    mm(ps_t[:, lo:width], ones[:, :], oh[:, 0:width - lo], start=False, stop=False,
                       skip_group_check=True)
                for t in range(TILES):
                    last = mm(ps_t[:, width:width + EXPERTS], ones[:, :], oh[:, t * EXPERTS:(t + 1) * EXPERTS],
                              start=False, stop=(t == TILES - 1), skip_group_check=True)
                last.then_inc(sem("rank_done"), 1)

            def chunk(it, att_on, ffn_on):
                f = it - 1
                for j in range(JT):
                    if ffn_on:
                        shared_in(f, j)
                        if j == 0:
                            route_in(f)
                        if j == 1:
                            route_rank(f)
                        if j >= 1:
                            shared_out(f, j - 1)
                    if att_on:
                        if 1 <= j <= TILES:
                            gram(it, j - 1, ffn_on)
                        if 2 <= j <= TILES + 1:
                            attend(it, j - 2)
                        if 3 <= j <= TILES + 2:
                            turn(it, j - 3)
                        if j < TILES:
                            project(it, j)
                if att_on:
                    out_linear(it)
                if ffn_on:
                    shared_out(f, JT - 1)

            chunk(0, True, False)
            pe.wait_ge(sem("shared_in"), 64)
            chunk(1, True, True)
            with pe.Fori(2, NCHUNK) as it:
                chunk(it, True, True)
            chunk(NCHUNK, False, True)

            pe.wait_ge(sem("expert_in"), 32 * EXPERTS)
            pe.wait_ge(sem("list_ready"), 2)
            pe.wait_ge(sem("base_ready"), NCHUNK)
            pe.wait_ge(sem("ys_ready"), TILES * NCHUNK)
            gu_flat = e_gu[:, :, :, :].rearrange("p e k f -> p (e k f)")
            dn_flat = e_down[:, :, :, :].rearrange("p e k f -> p (e k f)")

            def routed(g, u, first_body, last_body):
                i = UNROLL * g + u
                if not (last_body and u == UNROLL - 1):
                    n = u + 1
                    wait(pe, f"gat_in{n % UNROLL}", 16 * (g + 1 + n // UNROLL))
                    wait(pe, "rxT_ready", i)
                    for k in range(KT):
                        last = nc.tensor.transpose(bank[n % 2][:, k * P:(k + 1) * P],
                                                   gat[:, n % UNROLL, k * P:(k + 1) * P], ident)
                    last.then_inc(sem("rx_done"), 1)
                at = pe.value_load(woff[0:1, bass.ds(i, 1)], min_val=0, max_val=(EXPERTS - 1) * KT * F)
                wait(pe, "rxT_ready", i + 1)
                wait(pe, "rhid_ready", i - 1)
                for k in range(KT):
                    last = mm(bank[2 + u % 2][:, :], rxT[:, u % 2, k * P:(k + 1) * P],
                              gu_flat[:, bass.ds(at * 2 + k * 2 * EF, 2 * EF)], start=(k == 0), stop=(k == KT - 1))
                last.then_inc(sem("rgu_done"), 1)
                if not (first_body and u < 2):
                    routed_down(i - 2, u)
                if not (first_body and u < 1):
                    routed_turn(i - 1, u - 1)

            def routed_down(i, u):
                at = pe.value_load(woff[0:1, bass.ds(i, 1)], min_val=0, max_val=(EXPERTS - 1) * KT * F)
                wait(pe, "rhT_ready", i + 1)
                wait(pe, "res_ready", i - 1)
                for k in range(KT):
                    last = mm(bank[4 + u % 2][:, 0:F], rhT[:, u % 2, k * P:(k + 1) * P],
                              dn_flat[:, bass.ds(at + k * F, F)], start=(k == 0), stop=(k == KT - 1))
                last.then_inc(sem("rdown_done"), 1)

            def routed_turn(i, u):
                wait(pe, "rhid_ready", i + 1)
                wait(pe, "rhT_ready", i - 1)
                for k in range(KT):
                    last = nc.tensor.transpose(bank[6 + u % 2][:, k * P:(k + 1) * P],
                                               rhid[:, u % 2, k * P:(k + 1) * P], ident)
                last.then_inc(sem("rh_done"), 1)

            pe.wait_ge(sem("gat_in0"), 16)
            for k in range(KT):
                last = nc.tensor.transpose(bank[0][:, k * P:(k + 1) * P], gat[:, 0, k * P:(k + 1) * P], ident)
            last.then_inc(sem("rx_done"), 1)
            for u in range(UNROLL):
                routed(0, u, True, False)
            with pe.Fori(1, ROUTED // UNROLL - 1) as g:
                for u in range(UNROLL):
                    routed(g, u, False, False)
            for u in range(UNROLL):
                routed(ROUTED // UNROLL - 1, u, False, True)
            routed_down(ROUTED - 2, 0)
            routed_turn(ROUTED - 1, 1)
            routed_down(ROUTED - 1, 1)

        @block.scalar
        def _(act):
            dk = sc[0:BATCH, :, :].rearrange("p a b -> p (a b)")
            act.wait_ge(sem("sumsq_eps"), 1)
            nc.scalar.activation(dk[:, F:2 * F], dk[:, 0:F], ACT.Sqrt).then_inc(sem("sqrt_k"), 1)
            act.wait_ge(sem("sumsq_eps"), 2)
            nc.scalar.activation(aT[:, 1, 0:KT * BATCH], aT[:, 0, 0:KT * BATCH], ACT.Sqrt).then_inc(sem("sqrt_o"), 1)

            def aT_copy(it, t):
                wait(act, "turn_done", TILES * it + t + 1)
                if t == 0:
                    wait(act, "y_done", KT * it)
                    wait(act, "mod_ready", it + 1)
                for k in range(KT):
                    ins = nc.scalar.activation(aT[:, k, t * P:(t + 1) * P], ps_t[:, k * P:(k + 1) * P], ACT.Copy,
                                               scale=mod[:, KT + k, t // (TILES // CB):t // (TILES // CB) + 1])
                ins.then_inc(sem("aT_ready"), 1)

            def exps(it, t):
                wait(act, "s_taken", TILES * it + t + 1)
                nc.scalar.activation(sc[:, :, :], sc[:, :, :], ACT.Exp, scale=SCALE).then_inc(sem("exp_ready"), 1)

            def yT_copy(it):
                for o in range(KT):
                    wait(act, "y_done", KT * it + o + 1)
                    if o == 0:
                        wait(act, "up_done", JT * it)
                    for b in range(CB):
                        bk = (ps_k, ps_t)[o]
                        nc.scalar.activation(yT[:, o, b * SEQ:(b + 1) * SEQ], bk[:, b * SEQ:(b + 1) * SEQ],
                                             ACT.Identity, bias=biases[:, 2 * KT + o:2 * KT + o + 1],
                                             scale=mod[:, 2 * KT + o, b:b + 1]).then_inc(sem("yT_ready"), 1)

            def silus(f, j):
                wait(act, "gate_done", JT * f + j + 1)
                wait(act, "hid_ready", JT * f + j - 1)
                nc.scalar.activation(silu[:, j % 2, :], ps_gate[:, :], ACT.Silu).then_inc(sem("silu_ready"), 1)

            def score_exp(f):
                wait(act, "top_ready", f + 1)
                nc.scalar.activation(expt[:, :], top[:, :], ACT.Exp, scale=-1.0).then_inc(sem("expt_ready"), 1)

            def ys_copy(f):
                wait(act, "score_ready", f + 1)
                wait(act, "ys_out", 16 * f)
                for t in range(TILES):
                    wait(act, "yrow_done", TILES * f + 2 * (t // 2) + 2)
                    nc.scalar.activation(ys[:, t, :], (ps_s, ps_o)[t // 2][:, (t % 2) * F:(t % 2 + 1) * F], ACT.Copy,
                                         scale=score[:, t:t + 1]).then_inc(sem("ys_ready"), 1)

            def chunk(it, att_on, ffn_on):
                f = it - 1
                for j in range(JT):
                    if att_on and 4 <= j <= TILES + 3:
                        aT_copy(it, j - 4)
                    if att_on and 2 <= j <= TILES + 1:
                        exps(it, j - 2)
                    if ffn_on:
                        if j == 1:
                            ys_copy(f)
                        silus(f, j)
                        if j == 0:
                            score_exp(f)
                if att_on:
                    yT_copy(it)

            chunk(0, True, False)
            act.wait_ge(sem("filled"), 48)
            chunk(1, True, True)
            with act.Fori(2, NCHUNK) as it:
                chunk(it, True, True)
            chunk(NCHUNK, False, True)

            def rxT_copy(i, u):
                wait(act, "rx_done", i + 1)
                wait(act, "rgu_done", i - 1)
                nc.scalar.activation(rxT[:, u % 2, :], bank[u % 2][:, 0:KT * P], ACT.Copy)\
                    .then_inc(sem("rxT_ready"), 1)

            def routed(g, u, first_body, last_body):
                i = UNROLL * g + u
                if not (last_body and u == UNROLL - 1):
                    rxT_copy(i + 1, u + 1)
                wait(act, "rgu_done", i + 1)
                wait(act, "rhid_ready", i - 1)
                nc.scalar.activation(rsilu[:, u % 2, :], bank[2 + u % 2][:, 0:EF], ACT.Silu)\
                    .then_inc(sem("rsilu_ready"), 1)
                if not (first_body and u < 1):
                    rhT_copy(i - 1, u - 1)

            def rhT_copy(i, u):
                wait(act, "rh_done", i + 1)
                wait(act, "rdown_done", i - 1)
                nc.scalar.activation(rhT[:, u % 2, :], bank[6 + u % 2][:, 0:KT * P], ACT.Copy)\
                    .then_inc(sem("rhT_ready"), 1)

            rxT_copy(0, 0)
            for u in range(UNROLL):
                routed(0, u, True, False)
            with act.Fori(1, ROUTED // UNROLL - 1) as g:
                for u in range(UNROLL):
                    routed(g, u, False, False)
            for u in range(UNROLL):
                routed(ROUTED // UNROLL - 1, u, False, True)
            rhT_copy(ROUTED - 1, 1)

        @block.vector
        def _(dve):
            v = nc.vector
            dve.wait_ge(sem("consts_in"), 16)
            v.tensor_copy(tri[:, :], cst[:, C_TRI:C_TRI + P]).then_inc(sem("masks_ready"), 1)
            v.tensor_copy(mask_l[:, :], cst[0:2, C_ML:C_ML + P]).then_inc(sem("masks_ready"), 1)
            v.tensor_copy(mask_r[:, :], cst[0:2, C_MR:C_MR + PAIRS * 32]).then_inc(sem("masks_ready"), 1)
            v.tensor_copy(count[:, :], cst[:, C_BASE:C_BASE + EXPERTS]).then_inc(sem("count_ready"), 1)
            v.tensor_copy(tokid[:, :], cst[:, C_TOK:C_TOK + TILES]).then_inc(sem("tokid_ready"), 1)
            dve.wait_ge(sem("style_done"), 1)
            dve.wait_ge(sem("bias_in"), 32)
            for w in range(2 * KT):
                v.tensor_scalar(mods[:, :, w, :], ps_k[:, w * BATCH:(w + 1) * BATCH]
                                .rearrange("p (c b) -> p c b", b=CB), biases[:, w:w + 1], None, ALU.add)\
                    .then_inc(sem("styles_ready"), 1)
            dve.wait_ge(sem("styles_ready"), 2 * KT)
            sq = kpad[:, :, :, :].rearrange("p h s d -> p (h s d)")[:, 0:2 * KT * BATCH]\
                .rearrange("p (w c b) -> p w c b", w=2 * KT, b=CB)
            for w in range(2 * KT):
                v.tensor_tensor(sq[:, w], mods[:, :, w, :], mods[:, :, w, :], ALU.mult)\
                    .then_inc(sem("sq_part"), 1)
            dve.wait_ge(sem("wk_in"), 32)
            dve.wait_ge(sem("sq_part"), 2 * KT)
            for n, wt in enumerate((wk, wo)):
                flat = wt[:, :, :].rearrange("p k o -> p (k o)")
                v.tensor_tensor(keyT[:, n, :], flat, flat, ALU.mult).then_inc(sem("squares_ready"), 1)
            dk = sc[0:BATCH, :, :].rearrange("p a b -> p (a b)")
            tmp = probT[0:BATCH, 0, :]
            do_ = aT[:, 0, 0:KT * BATCH]
            so_ = aT[:, 1, 0:KT * BATCH]
            tmo = probT[:, 1, 0:KT * BATCH]
            dve.wait_ge(sem("sumsq_done"), 2)
            v.tensor_scalar(dk[:, 0:F], ps_s[0:BATCH, 0:F], EPS, None, ALU.add).then_inc(sem("sumsq_eps"), 1)
            v.tensor_scalar(do_, ps_o[:, 0:KT * BATCH], EPS, None, ALU.add).then_inc(sem("sumsq_eps"), 1)

            def newton(name, ready, total, root, t, dest):
                dve.wait_ge(sem(ready), 1)
                w_ = t.shape[-1] // 2
                a, b = t[:, 0:w_], t[:, w_:2 * w_]
                v.reciprocal(a, root).then_inc(sem(name), 1)
                dve.wait_ge(sem(name), 1)
                v.tensor_tensor(b, a, a, ALU.mult).then_inc(sem(name), 1)
                dve.wait_ge(sem(name), 2)
                v.tensor_tensor(b, b, total, ALU.mult).then_inc(sem(name), 1)
                dve.wait_ge(sem(name), 3)
                v.tensor_scalar(b, b, -0.5, 1.5, ALU.mult, ALU.add).then_inc(sem(name), 1)
                dve.wait_ge(sem(name), 4)
                return v.tensor_tensor(dest, a if len(dest.shape) == 2 else a.rearrange("p (c b) -> p c b", b=CB),
                                       b if len(dest.shape) == 2 else b.rearrange("p (c b) -> p c b", b=CB), ALU.mult)

            newton("newton_k", "sqrt_k", dk[:, 0:F], dk[:, F:2 * F], tmp, dk[:, F:2 * F]).then_inc(sem("demod_k"), 1)
            for o in range(KT):
                cols = slice(o * BATCH, (o + 1) * BATCH)
                newton(f"newton_o{o}", "sqrt_o", do_[:, cols], so_[:, cols],
                       probT[:, 1, 2 * o * BATCH:2 * (o + 1) * BATCH], mods[:, :, 2 * KT + o, :])\
                    .then_inc(sem("mods_ready"), 1)
            dve.wait_ge(sem("sumsq_done"), 2)
            v.memset(kpad[:, :, :, :], 1.0).then_inc(sem("kpad_set"), 1)
            dve.wait_ge(sem("kpad_set"), 1)
            dve.wait_ge(sem("mods_ready"), KT)
            dve.wait_ge(sem("ones_ready"), 1)
            dve.wait_ge(sem("demod_out"), 16)
            v.memset(rowmax[:, :], 0.0).then_inc(sem("masks_ready"), 1)

            def modulate(it):
                wait(dve, "yT_ready", KT * CB * it)
                wait(dve, "wkb_ready", it)
                v.tensor_copy(mod[:, :, :], mods[:, bass.ds(it, 1), :, :].rearrange("p c w b -> p (c w) b"))\
                    .then_inc(sem("mod_ready"), 1)
                wait(dve, "mod_ready", it + 1)
                wait(dve, "demod_in", 16 * (it + 1))
                wait(dve, "proj_done", TILES * it)
                for b in range(CB):
                    for k in range(KT):
                        ins = v.scalar_tensor_tensor(wkb[:, b, k, :], wk[:, k, :], mod[:, k, b:b + 1],
                                                     demod_b[:, b, :], ALU.mult, ALU.mult)
                ins.then_inc(sem("wkb_ready"), 1)

            def keys(it, t):
                wait(dve, "proj_done", TILES * it + t + 1)
                wait(dve, "keyT_ready", TILES * it + t)
                v.tensor_tensor(kpad[:, :, 0, :], ps_k[:, 0:F].rearrange("p (h d) -> p h d", h=HEADS),
                                bias_k[:, :].rearrange("p (h d) -> p h d", h=HEADS), ALU.add)\
                    .then_inc(sem("k_taken"), 1)
                wait(dve, "k_taken", TILES * it + t + 1)
                wait(dve, "gram_done", TILES * it + t - 1)
                wait(dve, "val_ready", TILES * it + t - 1)
                v.transpose(keyT[:, t % 2, :].rearrange("p (t h) -> p h t", h=HEADS),
                            kpad[:, :, :, :].rearrange("p h s d -> p h (s d)")).then_inc(sem("keyT_ready"), 1)
                wait(dve, "keyT_ready", TILES * it + t + 1)
                wait(dve, "av_done", TILES * it + t - 1)
                v.transpose(val[:, t % 2, :], keyT[:, t % 2, :]).then_inc(sem("val_ready"), 1)

            def soft(it, t):
                wait(dve, "gram_done", TILES * it + t + 1)
                wait(dve, "s_taken", TILES * it + t)
                scores = ps_s[:, :].rearrange("p (a b) -> p a b", b=32)
                v.tensor_reduce(rowmax[:, :], scores, AX.X, ALU.max).then_inc(sem("max_ready"), 1)
                wait(dve, "max_ready", TILES * it + t + 1)
                wait(dve, "probT_ready", TILES * it + t)
                v.tensor_tensor(sc[:, :, :], scores, rowmax[:, :].unsqueeze(2).to_broadcast([P, PAIRS, 32]),
                                ALU.subtract).then_inc(sem("s_taken"), 1)

            def soft_turn(it, t):
                wait(dve, "exp_ready", TILES * it + t + 1)
                wait(dve, "av_done", TILES * it + t - 1)
                v.transpose(probT[:, t % 2, :], sc[:, :, :].rearrange("p a b -> p (a b)"))\
                    .then_inc(sem("probT_ready"), 1)

            def normalise(it, t):
                wait(dve, "av_done", TILES * it + t + 1)
                wait(dve, "att_ready", TILES * it + t)
                v.transpose(ot[:, :, :, :].rearrange("p h s d -> p h (s d)"),
                            ps_o[:, :].rearrange("p (t h) -> p h t", h=HEADS)).then_inc(sem("o_taken"), 1)
                wait(dve, "o_taken", TILES * it + t + 1)
                v.reciprocal(rz[:, :], ot[:, :, 1, 0]).then_inc(sem("rz_ready"), 1)
                wait(dve, "rz_ready", TILES * it + t + 1)
                wait(dve, "turn_done", TILES * it + t)
                v.tensor_tensor(att[:, :].rearrange("p (h d) -> p h d", h=HEADS), ot[:, :, 0, :],
                                rz[:, :].unsqueeze(2).to_broadcast([P, HEADS, D]), ALU.mult)\
                    .then_inc(sem("att_ready"), 1)

            def hidden(f, j):
                wait(dve, "up_done", JT * f + j + 1)
                wait(dve, "silu_ready", JT * f + j + 1)
                wait(dve, "down_done", JT * f + j - 1)
                v.tensor_tensor(hid[:, j % 2, :], ps_up[:, :], silu[:, j % 2, :], ALU.mult)\
                    .then_inc(sem("hid_ready"), 1)

            def per_tile(a):
                return a.unsqueeze(2).to_broadcast([P, TILES, EXPERTS])

            def per_expert(a):
                return a.unsqueeze(1).to_broadcast([P, TILES, EXPERTS])

            def choose(f):
                logits = ps_t[:, 0:TILES * EXPERTS].rearrange("p (t e) -> p t e", e=EXPERTS)
                wait(dve, "logit_done", f + 1)
                wait(dve, "score_ready", f)
                wait(dve, "slot_ready", f)
                v.tensor_reduce(top[:, :], logits, AX.X, ALU.max).then_inc(sem("top_ready"), 1)
                wait(dve, "top_ready", f + 1)
                v.tensor_tensor(eq[:, :, :], logits, per_tile(top[:, :]), ALU.is_equal).then_inc(sem("eq_ready"), 1)
                wait(dve, "eq_ready", f + 1)
                v.tensor_tensor(pick[:, :, :], eq[:, :, :], per_expert(erev), ALU.mult).then_inc(sem("pick_ready"), 1)
                wait(dve, "pick_ready", f + 1)
                v.tensor_reduce(pickmax[:, :], pick[:, :, :], AX.X, ALU.max).then_inc(sem("pickmax_ready"), 1)
                wait(dve, "pickmax_ready", f + 1)
                v.tensor_tensor(onehot[:, :, :], pick[:, :, :], per_tile(pickmax[:, :]), ALU.is_equal)\
                    .then_inc(sem("onehot_ready"), 1)

            def score_of(f):
                wait(dve, "expt_ready", f + 1)
                wait(dve, "ys_ready", TILES * f)
                v.tensor_scalar(ex1[:, :], expt[:, :], 1.0, None, ALU.add).then_inc(sem("ex1_ready"), 1)
                wait(dve, "ex1_ready", f + 1)
                v.reciprocal(score[:, :], ex1[:, :]).then_inc(sem("score_ready"), 1)

            def place(f, first_chunk):
                width = TILES * EXPERTS
                wait(dve, "rank_done", f + 1)
                wait(dve, "count_ready", f + 1)
                v.tensor_tensor(rank[:, :, :], ps_t[:, 0:width].rearrange("p (t e) -> p t e", e=EXPERTS),
                                per_expert(count[:, :]), ALU.add).then_inc(sem("rank_ready"), 1)
                wait(dve, "rank_ready", f + 1)
                v.tensor_tensor(count[:, :], count[:, :], ps_t[:, width:width + EXPERTS], ALU.add)\
                    .then_inc(sem("count_ready"), 1)
                wait(dve, "count_ready", f + 2)
                v.tensor_tensor(slotsel[:, :, :], rank[:, :, :], onehot[:, :, :], ALU.mult)\
                    .then_inc(sem("rank_taken"), 1)
                wait(dve, "rank_taken", f + 1)
                v.tensor_reduce(slotf[:, :], slotsel[:, :, :], AX.X, ALU.add).then_inc(sem("slotf_ready"), 1)
                wait(dve, "slotf_ready", f + 1)
                if not first_chunk:
                    wait(dve, "slots_out", 16 * TILES * f)
                    wait(dve, "tokid_ready", f)
                    v.tensor_scalar(tokid[:, :], tokid[:, :], float(CHUNK), None, ALU.add)\
                        .then_inc(sem("tokid_ready"), 1)
                wait(dve, "tokid_ready", f + 1)
                v.tensor_copy(slot[:, :], slotf[:, :]).then_inc(sem("slot_ready"), 1)

            def sum_rows(f):
                wait(dve, "down_done", JT * (f + 1))
                wait(dve, "xr_in", 16 * (f + 1))
                wait(dve, "base_out", 16 * f)
                for n, bk in enumerate((ps_sh0, ps_sh1)):
                    ins = v.tensor_tensor(base[:, 2 * n:2 * n + 2, :], bk[:, :].rearrange("p (t f) -> p t f", f=F),
                                          xr[:, 2 * n:2 * n + 2, :], ALU.add)
                ins.then_inc(sem("base_ready"), 1)

            def chunk(it, att_on, ffn_on, first_ffn=False):
                f = it - 1
                if att_on:
                    modulate(it)
                for j in range(JT):
                    if ffn_on and j == 0:
                        choose(f)
                    if ffn_on and j == 1:
                        score_of(f)
                        place(f, first_ffn)
                    if att_on:
                        if 2 <= j <= TILES + 1:
                            soft(it, j - 2)
                        if 1 <= j <= TILES:
                            keys(it, j - 1)
                        if 2 <= j <= TILES + 1:
                            soft_turn(it, j - 2)
                        if 3 <= j <= TILES + 2:
                            normalise(it, j - 3)
                    if ffn_on:
                        hidden(f, j)
                if ffn_on:
                    sum_rows(f)

            chunk(0, True, False)
            dve.wait_ge(sem("filled"), 48)
            chunk(1, True, True, True)
            with dve.Fori(2, NCHUNK) as it:
                chunk(it, True, True)
            chunk(NCHUNK, False, True)

            step = [0]

            def link(ins):
                step[0] += 1
                ins.then_inc(sem("list_step"), 1)
                dve.wait_ge(sem("list_step"), step[0])

            dve.wait_ge(sem("count_ready"), NCHUNK + 1)
            NK = TOKENS // P
            link(v.tensor_tensor(held[:, :], count[0:1, :], cst[0:1, C_BASE:C_BASE + EXPERTS], ALU.subtract))
            link(v.tensor_tensor(more[:, :, :], held[:, :].unsqueeze(2).to_broadcast([1, EXPERTS, NK]),
                                 cst[0:1, C_STEP:C_STEP + NK].unsqueeze(1).to_broadcast([1, EXPERTS, NK]), ALU.is_gt))
            link(v.tensor_reduce(ntile[:, :], more[:, :, :], AX.X, ALU.add))
            link(v.memset(held[:, :], 1.0))
            link(v.tensor_tensor_scan(tend[:, :], held[:, :], ntile[:, :], 0.0, ALU.mult, ALU.add))
            numbers = cst[0:1, C_TILE:C_TILE + ROUTED]
            link(v.tensor_tensor(before[:, :, :], tend[:, :].unsqueeze(1).to_broadcast([1, ROUTED, EXPERTS]),
                                 numbers.unsqueeze(2).to_broadcast([1, ROUTED, EXPERTS]), ALU.is_le))
            link(v.tensor_reduce(which[:, :], before[:, :, :], AX.X, ALU.add))
            link(v.tensor_tensor(weighed[:, :, :], before[:, :, :],
                                 ntile[:, :].unsqueeze(1).to_broadcast([1, ROUTED, EXPERTS]), ALU.mult))
            link(v.tensor_reduce(first[:, :], weighed[:, :, :], AX.X, ALU.add))
            link(v.tensor_tensor(within[:, :], numbers, first[:, :], ALU.subtract))
            link(v.tensor_scalar(within[:, :], within[:, :], float(P), None, ALU.mult))
            link(v.scalar_tensor_tensor(offf[:, :], which[:, :], float(TOKENS), within[:, :], ALU.mult, ALU.add))
            v.tensor_copy(off[:, :], offf[:, :]).then_inc(sem("list_ready"), 1)
            link(v.tensor_scalar(wofff[:, :], which[:, :], float(EXPERTS - 1), float(KT * F), ALU.min, ALU.mult))
            v.tensor_copy(woff[:, :], wofff[:, :]).then_inc(sem("list_ready"), 1)

            def rhidden(g, u, first_body):
                i = UNROLL * g + u
                wait(dve, "rgu_done", i + 1)
                wait(dve, "rsilu_ready", i + 1)
                wait(dve, "rh_done", i - 1)
                v.tensor_tensor(rhid[:, u % 2, :], bank[2 + u % 2][:, EF:2 * EF], rsilu[:, u % 2, :], ALU.mult)\
                    .then_inc(sem("rhid_ready"), 1)
                if not (first_body and u < 2):
                    result(i - 2, u - 2, g if u >= 2 else g - 1)

            def result(i, u, g):
                wait(dve, "rdown_done", i + 1)
                wait(dve, f"res_out{u % UNROLL}", 16 * g)
                v.tensor_tensor(res[:, u % UNROLL, :], bank[4 + u % 2][:, 0:F], gat[:, u % UNROLL, F:2 * F], ALU.add)\
                    .then_inc(sem("res_ready"), 1)

            for u in range(UNROLL):
                rhidden(0, u, True)
            with dve.Fori(1, ROUTED // UNROLL) as g:
                for u in range(UNROLL):
                    rhidden(g, u, False)
            for u in (UNROLL - 2, UNROLL - 1):
                result(ROUTED - UNROLL + u, u, ROUTED // UNROLL - 1)


NAMES = ["xT", "x", "condT", "k_affT", "k_wT", "k_b", "o_affT", "o_wT", "bias_cols", "routerT",
         "gate_up", "down", "sh_gateT", "sh_upT", "sh_downT", "consts"]


def constants(np):
    c = np.zeros((P, C_END), np.float32)
    i = np.arange(P)
    c[:, C_ID:C_ID + P] = np.eye(P)
    c[:, C_TRI:C_TRI + P] = i[:, None] < i[None, :]
    for r in range(2):
        c[r, C_ML:C_ML + P] = (i // HEADS) % 2 == r
        c[r, C_MR:C_MR + PAIRS * 32] = np.where((np.arange(PAIRS * 32) // HEADS) % 2 == r, 0.0, MASKED)
    c[:, C_REV:C_REV + EXPERTS] = EXPERTS - np.arange(EXPERTS)
    c[:, C_BASE:C_BASE + EXPERTS] = TOKENS * np.arange(EXPERTS)
    c[:, C_STEP:C_STEP + TOKENS // P] = P * np.arange(TOKENS // P)
    c[:, C_TILE:C_TILE + ROUTED] = np.arange(ROUTED)
    c[:, C_TOK:C_TOK + TILES] = i[:, None] + P * np.arange(TILES)[None, :]
    return c


def kernel(x, cond_512, L0_cond_k_aff_w, L0_cond_k_aff_b, L0_cond_k_w, L0_cond_k_b, L0_cond_o_aff_w,
           L0_cond_o_aff_b, L0_cond_o_w, L0_cond_o_b, L0_ffn_router_w, L0_ffn_gate_up_proj, L0_ffn_down_proj,
           L0_ffn_shared_gate_w, L0_ffn_shared_up_w, L0_ffn_shared_down_w):
    import numpy as np
    import concourse.bacc as bacc
    from concourse.bass_utils import run_bass_kernel_spmd

    flat = np.ascontiguousarray(x).reshape(TOKENS, F)
    data = dict(
        xT=flat.reshape(NCHUNK, CHUNK, KT, P).transpose(0, 3, 2, 1),
        x=flat.reshape(TOKENS // P, P, F),
        condT=np.asarray(cond_512).T,
        k_affT=np.asarray(L0_cond_k_aff_w).T, k_wT=np.asarray(L0_cond_k_w).T, k_b=L0_cond_k_b,
        o_affT=np.asarray(L0_cond_o_aff_w).T, o_wT=np.asarray(L0_cond_o_w).T,
        bias_cols=np.stack([np.asarray(b).reshape(KT, P).T
                            for b in (L0_cond_k_aff_b, L0_cond_o_aff_b, L0_cond_o_b)], axis=1).reshape(P, 3 * KT),
        routerT=np.asarray(L0_ffn_router_w).T, gate_up=L0_ffn_gate_up_proj, down=L0_ffn_down_proj,
        sh_gateT=np.asarray(L0_ffn_shared_gate_w).T, sh_upT=np.asarray(L0_ffn_shared_up_w).T,
        sh_downT=np.asarray(L0_ffn_shared_down_w).T, consts=constants(np),
    )
    nc = bacc.Bacc("TRN2", target_bir_lowering=False, num_devices=1)
    arrays, args = {}, []
    for name in NAMES:
        a = np.ascontiguousarray(data[name])
        arrays["in_" + name] = a
        args.append(nc.dram_tensor("in_" + name, a.shape, mybir.dt.from_np(a.dtype), kind="ExternalInput").ap())
    out = nc.dram_tensor("out_rows", (TOKENS, F), F32, kind="ExternalOutput").ap()
    build_program(nc, *args, out)
    r = run_bass_kernel_spmd(nc, [arrays], core_ids=[0])
    return r.results[0]["out_rows"].reshape(BATCH, SEQ, F)
```

```python
from contextlib import ExitStack

import concourse.bass as bass
from concourse import mybir

F32 = mybir.dt.float32
F32R = mybir.dt.float32r
BF16 = mybir.dt.bfloat16
I32 = mybir.dt.int32
ALU = mybir.AluOpType
ACT = mybir.ActivationFunctionType
AX = mybir.AxisListType

P = 128
BATCH, SEQ, F = 32, 256, 256
COND = 128
HEADS, D = 16, 16
EXPERTS, EF = 16, 256
SF = 1024
TOKENS = BATCH * SEQ
KT = F // P
CHUNK = 512
TILES = CHUNK // P
CB = CHUNK // SEQ
NCHUNK = TOKENS // CHUNK
Q = 4
PAIRS = 16
JT = SF // P
NMOD = 6
ROUTED = TOKENS // P + EXPERTS
LEAD = 7
SPLITS = 4
UNROLL = 10
TABLE = EXPERTS * TOKENS + ROUTED * P
EMPTY = TOKENS
LATE_GU = 2
LATE_DOWN = 4
EPS = 1e-8
SCALE = 1.0 / D ** 0.5

C_ID = 0
C_TRI = C_ID + P
C_PAR = C_TRI + P
C_REV = C_PAR + 2
C_BASE = C_REV + EXPERTS
C_STEP = C_BASE + EXPERTS
C_TILE = C_STEP + TOKENS // P
C_TOK = C_TILE + ROUTED
C_END = C_TOK + TILES
ARENA = UNROLL * 2 * F + 8 * F + UNROLL * F


def build_program(nc, xT, x, condT, k_affT, k_wT, k_b, o_affT, o_wT, bias_cols, routerT,
                  gate_up, down, sh_gateT, sh_upT, sh_downT, consts, out):
    demod_rows = nc.dram_tensor("demod_rows", [BATCH, F], F32).ap()
    slot_table = nc.dram_tensor("slot_table", [TABLE, 1], I32).ap()
    rows = nc.dram_tensor("routed_rows", [TOKENS + 1, 2 * F], F32).ap()

    ctx = ExitStack()
    with ctx:
        def sb(name, shape, dt=F32):
            return ctx.enter_context(nc.sbuf_tensor("sb_" + name, shape, dt))

        made = {}
        passed = {nc.sync: "loads_passed", nc.gpsimd: "indirect_passed"}

        def sem(name):
            if name not in made:
                made[name] = ctx.enter_context(nc.semaphore(name))
            return made[name]

        def wait(eng, name, n):
            if not isinstance(n, int) or n > 0:
                eng.wait_ge(sem(name), n)
            if not isinstance(n, int) and eng in passed:
                eng.sem_inc(sem(passed[eng]), 1)

        cst = sb("consts", [P, C_END])
        tri = sb("tri", [P, P], BF16)
        ones = sb("ones", [P, P], BF16)
        wk = sb("wk", [P, KT, F])
        wo = sb("wo", [P, KT, F])
        w_router = sb("w_router", [P, KT, EXPERTS])
        gate_hi = sb("gate_hi", [P, KT, SF], F32R)
        up_hi = sb("up_hi", [P, KT, SF], F32R)
        w_down = sb("w_down", [P, JT, F])
        gu_base = nc.sbuf_base
        e_gu = sb("e_gu", [P, EXPERTS, KT, 2 * EF])
        down_base = nc.sbuf_base
        e_down = sb("e_down", [P, EXPERTS, KT, F])
        gate_lo = nc.alloc_sbuf_tensor_at("sb_gate_lo", [P, KT, SF], F32R,
                                          offset=gu_base + (EXPERTS - LATE_GU) * KT * 2 * EF * 4)
        up_lo = nc.alloc_sbuf_tensor_at("sb_up_lo", [P, KT, SF], F32R,
                                        offset=down_base + (EXPERTS - LATE_DOWN) * KT * F * 4)
        bias_k = sb("bias_k", [P, F])
        bias_kp = sb("bias_kp", [P, 2, F])
        biases = sb("biases", [P, 3 * KT])
        mods = sb("mods", [P, NCHUNK, NMOD, CB])
        mod = sb("mod", [P, NMOD, CB])
        arena = sb("arena", [P, ARENA])
        taken = [0]

        def part(*shape):
            n = 1
            for m in shape:
                n *= m
            lo = taken[0]
            taken[0] += n
            ap = arena[:, lo:lo + n]
            names = "abc"[:len(shape)]
            if len(shape) > 1:
                ap = ap.rearrange(f"p ({' '.join(names)}) -> p {' '.join(names)}", **dict(zip(names[1:], shape[1:])))
            return ap

        xt = part(KT, CHUNK)
        wkb = part(CB, KT, F)
        kpad = part(HEADS, 2, D)
        keyT = part(2, 32 * HEADS)
        val = part(2, PAIRS * 32)
        keysum = part(2, PAIRS * HEADS)
        sc = part(32, HEADS)
        probT = part(2, PAIRS * 32)
        ot = part(D, 32)
        att = part(HEADS * D)
        aT = part(KT, CHUNK)
        demod_b = sb("demod_b", [P, CB, F])
        rowmax = sb("rowmax", [P, 32])
        z = sb("z", [P, 32])
        zT = sb("zT", [P, 32])
        rz = sb("rz", [P, 2, HEADS])
        yT = sb("yT", [P, KT, CHUNK])
        y_hi = sb("y_hi", [P, KT, CHUNK], F32R)
        y_lo = sb("y_lo", [P, KT, CHUNK], F32R)
        silu = sb("silu", [P, 2, CHUNK])
        hid = sb("hid", [P, 2, CHUNK])
        base = sb("base", [P, TILES, F])
        ys = sb("ys", [P, TILES, F])
        top = sb("top", [P, TILES])
        expt = sb("expt", [P, TILES])
        ex1 = sb("ex1", [P, TILES])
        score = sb("score", [P, TILES])
        eq = sb("eq", [P, TILES, EXPERTS])
        pick = sb("pick", [P, TILES, EXPERTS])
        pickmax = sb("pickmax", [P, TILES])
        onehot = sb("onehot", [P, TILES, EXPERTS], BF16)
        rank = sb("rank", [P, TILES, EXPERTS])
        slotsel = sb("slotsel", [P, TILES, EXPERTS])
        slotf = sb("slotf", [P, TILES])
        slot = sb("slot", [P, TILES], I32)
        tokid = sb("tokid", [P, TILES], I32)
        count = sb("count", [P, EXPERTS])
        held = sb("held", [1, EXPERTS])
        ntile = sb("ntile", [1, EXPERTS])
        tend = sb("tend", [1, EXPERTS])
        which = sb("which", [1, ROUTED])
        first = sb("first", [1, ROUTED])
        within = sb("within", [1, ROUTED])
        offf = sb("offf", [1, ROUTED])
        wofff = sb("wofff", [1, ROUTED])
        off = sb("off", [1, ROUTED], I32)
        woff = sb("woff", [1, ROUTED], I32)
        idx = sb("idx", [P, UNROLL], I32)
        taken[0] = 0
        gat = part(UNROLL, 2 * F)
        rxT = part(2, KT * P)
        rsilu = part(2, EF)
        rhid = part(2, EF)
        rhT = part(2, KT * P)
        res = part(UNROLL, F)
        taken[0] = 0
        more = part(EXPERTS, TOKENS // P)[0:1]
        before = part(ROUTED, EXPERTS)[0:1]
        weighed = part(ROUTED, EXPERTS)[0:1]

        bank = [ctx.enter_context(nc.psum_tensor(f"bank{i}", [P, 512], F32)) for i in range(8)]
        ps_gate, ps_up, ps_sh0, ps_sh1, ps_k, ps_s, ps_o, ps_t = bank
        ident = cst[:, C_ID:C_ID + P]
        erev = cst[:, C_REV:C_REV + EXPERTS]
        parity = cst[:, C_PAR:C_PAR + 2]

        def modview(w0, w1):
            return mods[:, :, w0:w1, :]

        whole_gate, whole_up = (e_gu[:, 10 + 2 * n:12 + 2 * n, :, :].rearrange("p e k f -> p (e k f)")
                                .rearrange("p (k o) -> p k o", k=KT) for n in range(2))

        block = ctx.enter_context(nc.Block())

        @block.sync
        def _(sp):
            sp.dma_start(cst[:, :], consts).then_inc(sem("consts_in"), 16)
            sp.dma_start(ot[:, :, :].rearrange("p d h -> p (d h)")[:, 0:BATCH], condT)\
                .then_inc(sem("cond_in"), 16)
            sp.dma_start(att[:, 0:F], k_affT).then_inc(sem("cond_in"), 16)
            sp.dma_start(sc[:, :, :].rearrange("p a b -> p (a b)")[:, 0:F], o_affT).then_inc(sem("cond_in"), 16)
            sp.dma_start(wk[:, :, :], k_wT.rearrange("(k p) o -> p k o", p=P)).then_inc(sem("wk_in"), 16)
            sp.dma_start(wo[:, :, :], o_wT.rearrange("(k p) o -> p k o", p=P)).then_inc(sem("wk_in"), 16)
            sp.dma_start(biases[:, :], bias_cols).then_inc(sem("bias_in"), 16)
            sp.dma_start(bias_k[:, :], k_b.partition_broadcast(P)).then_inc(sem("bias_in"), 16)
            sp.dma_start(xt[:, :, :], xT[0, :, :, :]).then_inc(sem("xt_in"), 16)
            sp.dma_start(whole_gate, sh_gateT.rearrange("(k p) o -> p k o", p=P)).then_inc(sem("shared_in"), 16)
            sp.dma_start(whole_up, sh_upT.rearrange("(k p) o -> p k o", p=P)).then_inc(sem("shared_in"), 16)
            sp.dma_start(w_down[:, :, :], sh_downT.rearrange("(j p) o -> p j o", p=P)).then_inc(sem("shared_in"), 16)
            sp.dma_start(w_router[:, :, :], routerT.rearrange("(k p) o -> p k o", p=P)).then_inc(sem("shared_in"), 16)
            sp.wait_ge(sem("fill_ready"), 2)
            fill = ys[:, :, :].rearrange("p t f -> p (t f)").bitcast(I32)
            whole = EXPERTS * TOKENS
            sp.dma_start(slot_table[0:whole, :].rearrange("(p t) o -> p (t o)", p=P), fill)\
                .then_inc(sem("filled"), 16)
            sp.dma_start(slot_table[whole:TABLE, :].rearrange("(p t) o -> p (t o)", p=P), fill[:, 0:ROUTED])\
                .then_inc(sem("filled"), 16)
            sp.dma_start(rows[TOKENS:TOKENS + 1, :], base[0:1, 0:2, :].rearrange("p t f -> p (t f)"))\
                .then_inc(sem("filled"), 16)
            sp.wait_ge(sem("demod_k"), 1)
            sp.dma_start(demod_rows, sc[0:BATCH, :, :].rearrange("p a b -> p (a b)")[:, F:2 * F])\
                .then_inc(sem("demod_out"), 16)
            sp.wait_ge(sem("demod_out"), 16)
            sp.dma_start(demod_b[:, :, :], demod_rows[0:CB, :].partition_broadcast(P)).then_inc(sem("demod_in"), 16)

            def load_experts(lo, n, wide, deep):
                if wide:
                    sp.dma_start(e_gu[:, bass.ds(lo, n), :, :].rearrange("p e k f -> p (e k) f"),
                                 gate_up[bass.ds(lo, n), :, :].rearrange("e (k p) f -> p (e k) f", p=P))\
                        .then_inc(sem("expert_in"), 16)
                if deep:
                    sp.dma_start(e_down[:, bass.ds(lo, n), :, :].rearrange("p e k f -> p (e k) f"),
                                 down[bass.ds(lo, n), :, :].rearrange("e (k p) f -> p (e k) f", p=P))\
                        .then_inc(sem("expert_in"), 16)

            def chunk(it, att_on, ffn_on, ahead, wide=False, deep=False):
                if ffn_on:
                    wait(sp, "base_out", 16 * (it - 1))
                    sp.dma_start(base[:, :, :], x[bass.ds((it - 1) * TILES, TILES), :, :].rearrange("t p f -> p t f"))\
                        .then_inc(sem("residual_in"), 16)
                if ahead:
                    wait(sp, "wkb_ready", it + 1)
                    sp.dma_start(demod_b[:, :, :],
                                 demod_rows[bass.ds((it + 1) * CB, CB), :].partition_broadcast(P))\
                        .then_inc(sem("demod_in"), 16)
                if ffn_on:
                    wait(sp, "ys_ready", TILES * it)
                    sp.dma_start(rows[bass.ds((it - 1) * CHUNK, CHUNK), 0:F].rearrange("(t p) f -> p t f", p=P),
                                 ys[:, :, :]).then_inc(sem("ys_out"), 16)
                if ahead:
                    wait(sp, "proj_done", TILES * (it + 1))
                    sp.dma_start(xt[:, :, :], xT[bass.ds(it + 1, 1), :, :, :].rearrange("a p k t -> p (a k) t"))\
                        .then_inc(sem("xt_in"), 16)
                load_experts(it, 1, wide, deep)
                if ffn_on and not att_on:
                    sp.wait_ge(sem("up_done"), JT * NCHUNK)
                    load_experts(EXPERTS - LATE_GU, LATE_GU, True, False)
                    load_experts(EXPERTS - LATE_DOWN, LATE_DOWN, False, True)
                if ffn_on:
                    wait(sp, "base_ready", it)
                    sp.dma_start(rows[bass.ds((it - 1) * CHUNK, CHUNK), F:2 * F].rearrange("(t p) f -> p t f", p=P),
                                 base[:, :, :]).then_inc(sem("base_out"), 16)

            chunk(0, True, False, True, True, True)
            sp.wait_ge(sem("filled"), 48)
            chunk(1, True, True, True, True, True)
            sp.wait_ge(sem("weights_lo"), 2 * SPLITS)
            with sp.Fori(2, EXPERTS - LATE_DOWN) as it:
                chunk(it, True, True, True, True, True)
            for it in range(EXPERTS - LATE_DOWN, NCHUNK):
                chunk(it, True, True, it < NCHUNK - 1, it < EXPERTS - LATE_GU, False)
            chunk(NCHUNK, False, True, False)
            sp.wait_ge(sem("slots_out"), 16 * TILES * NCHUNK)
            sp.wait_ge(sem("list_ready"), 2)
            with sp.Fori(0, ROUTED // UNROLL) as g:
                for u in range(UNROLL):
                    at = sp.value_load(off[0:1, bass.ds(UNROLL * g + u, 1)], min_val=0, max_val=TABLE - P)
                    wait(sp, f"res_out{u}", 16 * g)
                    sp.dma_start(idx[:, u:u + 1], slot_table[bass.ds(at, P), :]).then_inc(sem(f"idx_in{u}"), 16)

        @block.gpsimd
        def _(pool):
            pool.memset(ys[:, :, :].rearrange("p t f -> p (t f)").bitcast(I32), EMPTY).then_inc(sem("fill_ready"), 1)
            pool.memset(base[0:1, 0:2, :], 0.0).then_inc(sem("fill_ready"), 1)
            pool.memset(ones[:, :], 1.0).then_inc(sem("ones_ready"), 1)

            def scatter_ids(f):
                wait(pool, "slot_ready", f + 1)
                for t in range(TILES):
                    pool.indirect_dma_start(slot_table[:, :], bass.IndirectOffsetOnAxis(slot[:, t:t + 1], 0),
                                            tokid[:, t:t + 1], None, bounds_check=TABLE - 1, oob_is_err=False)\
                        .then_inc(sem("slots_out"), 16)

            with pool.Fori(0, NCHUNK) as f:
                scatter_ids(f)

            pool.wait_ge(sem("ys_out"), 16 * NCHUNK)
            pool.wait_ge(sem("base_out"), 16 * NCHUNK)

            def gather(g, u):
                wait(pool, f"idx_in{u}", 16 * (g + 1))
                pool.indirect_dma_start(gat[:, u, :], None, rows[:, :],
                                        bass.IndirectOffsetOnAxis(idx[:, u:u + 1], 0), bounds_check=TOKENS, oob_is_err=False)\
                    .then_inc(sem(f"gat_in{u}"), 16)

            def scatter(g, u):
                wait(pool, "res_ready", g * UNROLL + u + 1)
                pool.indirect_dma_start(out, bass.IndirectOffsetOnAxis(idx[:, u:u + 1], 0),
                                        res[:, u, :], None, bounds_check=TOKENS - 1, oob_is_err=False)\
                    .then_inc(sem(f"res_out{u}"), 16)

            last = ROUTED // UNROLL - 1

            def step(g, u, last_body):
                if not (last_body and u + LEAD >= UNROLL):
                    gather(g + (u + LEAD) // UNROLL, (u + LEAD) % UNROLL)
                scatter(g, u)

            pool.wait_ge(sem("filled"), 48)
            for u in range(LEAD):
                gather(0, u)
            for u in range(UNROLL):
                step(0, u, False)
            with pool.Fori(1, last) as g:
                for u in range(UNROLL):
                    step(g, u, False)
            for u in range(UNROLL):
                step(last, u, True)
            for u in range(UNROLL):
                pool.wait_ge(sem(f"res_out{u}"), 16 * (last + 1))

        @block.tensor
        def _(pe):
            mm = nc.tensor.matmul
            cond = ot[:, :, :].rearrange("p d h -> p (d h)")[:, 0:BATCH]
            affo = sc[:, :, :].rearrange("p a b -> p (a b)")[:, 0:F]
            pe.wait_ge(sem("cond_in"), 48)
            for w in range(2 * KT):
                src = att[:, (w % KT) * P:(w % KT + 1) * P] if w < KT else affo[:, (w % KT) * P:(w % KT + 1) * P]
                last = mm(ps_k[:, w * BATCH:(w + 1) * BATCH], src, cond, start=True, stop=True)
            last.then_inc(sem("style_done"), 1)
            pe.wait_ge(sem("squares_ready"), 2)
            sq = kpad[:, :, :, :].rearrange("p h s d -> p (h s d)")
            w2 = keyT[:, :, :]
            for k in range(KT):
                last = mm(ps_s[0:BATCH, 0:F], sq[:, k * BATCH:(k + 1) * BATCH], w2[:, 0, k * F:(k + 1) * F],
                          start=(k == 0), stop=(k == KT - 1))
            last.then_inc(sem("sumsq_done"), 1)
            for o in range(KT):
                for k in range(KT):
                    last = mm(ps_o[:, o * BATCH:(o + 1) * BATCH], w2[:, 1, k * F + o * P:k * F + (o + 1) * P],
                              sq[:, (KT + k) * BATCH:(KT + k + 1) * BATCH], start=(k == 0), stop=(k == KT - 1))
            last.then_inc(sem("sumsq_done"), 1)

            def project(it, t):
                wait(pe, "wkb_ready", it + 1)
                if t == 0:
                    wait(pe, "xt_in", 16 * (it + 1))
                    wait(pe, "yT_ready", KT * CB * it)
                wait(pe, "k_taken", 2 * (TILES * it + t))
                for k in range(KT):
                    last = mm(ps_k[:, 0:F], xt[:, k, t * P:(t + 1) * P], wkb[:, t // (TILES // CB), k, :],
                              start=(k == 0), stop=(k == KT - 1))
                last.then_inc(sem("proj_done"), 1)

            def gram(it, t, ffn_on):
                pe.wait_ge(sem("banks_set"), 2)
                wait(pe, "keysum_ready", TILES * it + t + 1)
                wait(pe, "s_taken", TILES * it + t)
                if t == 0 and ffn_on:
                    wait(pe, "ys_ready", TILES * it)
                pe.sem_inc(sem("products_passed"), 1)
                for pr in range(PAIRS):
                    for q in range(Q):
                        last = mm(ps_s[32 * q:32 * q + HEADS, 32 * pr:32 * pr + 32],
                                  keysum[32 * q:32 * q + 32, t % 2, HEADS * pr:HEADS * (pr + 1)],
                                  keyT[32 * q:32 * q + 32, t % 2, 32 * pr:32 * pr + 32],
                                  start=True, stop=True, tile_position=(32 * q, 32 * q), skip_group_check=True)
                last.then_inc(sem("gram_done"), 1)

            def attend(it, t):
                pe.wait_ge(sem("banks_set"), 2)
                wait(pe, "probT_ready", TILES * it + t + 1)
                wait(pe, "o_taken", TILES * it + t)
                for pr in range(PAIRS):
                    for q in range(Q):
                        last = mm(ps_o[32 * q:32 * q + HEADS, 32 * pr:32 * pr + 32],
                                  probT[32 * q:32 * q + 32, t % 2, 32 * pr:32 * pr + HEADS],
                                  val[32 * q:32 * q + 32, t % 2, 32 * pr:32 * pr + 32],
                                  start=True, stop=True, tile_position=(32 * q, 32 * q), skip_group_check=True)
                last.then_inc(sem("av_done"), 1)

            def turn(it, t):
                wait(pe, "att_ready", TILES * it + t + 1)
                if t == 0:
                    wait(pe, "rank_taken", it)
                    wait(pe, "yT_ready", KT * CB * it)
                wait(pe, "aT_ready", TILES * it + t)
                for k in range(KT):
                    last = nc.tensor.transpose(ps_t[:, k * P:(k + 1) * P], att[:, k * P:(k + 1) * P], ident)
                last.then_inc(sem("turn_done"), 1)

            def out_linear(it):
                wait(pe, "aT_ready", TILES * (it + 1))
                for o in range(KT):
                    bk = (ps_k, ps_t)[o]
                    for k in range(KT):
                        last = mm(bk[:, :], wo[:, k, o * P:(o + 1) * P], aT[:, k, :], start=(k == 0),
                                  stop=(k == KT - 1))
                    last.then_inc(sem("y_done"), 1)

            def shared_in(f, j):
                if j == 0:
                    wait(pe, "y_hi_ready", KT * (f + 1))
                    wait(pe, "y_lo_ready", KT * (f + 1))
                wait(pe, "silu_ready", JT * f + j)
                for hi, lo, bk, name in ((gate_hi, gate_lo, ps_gate, "gate_done"), (up_hi, up_lo, ps_up, "up_done")):
                    if name == "up_done":
                        wait(pe, "hid_ready", JT * f + j)
                    cols = slice(j * P, (j + 1) * P)
                    for k in range(KT):
                        mm(bk[:, :], hi[:, k, cols], y_hi[:, k, :], start=(k == 0), stop=False)
                        mm(bk[:, :], hi[:, k, cols], y_lo[:, k, :], start=False, stop=False)
                        last = mm(bk[:, :], lo[:, k, cols], y_hi[:, k, :], start=False, stop=(k == KT - 1))
                    last.then_inc(sem(name), 1)

            def shared_out(f, j):
                wait(pe, "hid_ready", JT * f + j + 1)
                if j == 0:
                    wait(pe, "base_ready", f)
                for t in range(TILES):
                    bk = (ps_sh0, ps_sh1)[t // 2]
                    last = mm(bk[:, (t % 2) * F:(t % 2 + 1) * F], hid[:, j % 2, t * P:(t + 1) * P],
                              w_down[:, j, :], start=(j == 0 and t % 2 == 0), stop=(j == JT - 1),
                              skip_group_check=True)
                last.then_inc(sem("down_done"), 1)

            def route_in(f):
                wait(pe, "yT_ready", KT * CB * (f + 1))
                wait(pe, "aT_ready", TILES * (f + 1))
                for t in range(TILES):
                    for k in range(KT):
                        last = mm(ps_t[:, t * EXPERTS:(t + 1) * EXPERTS], yT[:, k, t * P:(t + 1) * P],
                                  w_router[:, k, :], start=(k == 0), stop=(k == KT - 1), skip_group_check=True)
                last.then_inc(sem("logit_done"), 1)
                wait(pe, "s_taken", TILES * (f + 1))
                wait(pe, "o_taken", TILES * (f + 1))
                for t in range(TILES):
                    bk = (ps_s, ps_o)[t // 2]
                    for k in range(KT):
                        last = nc.tensor.transpose(bk[:, (t % 2) * F + k * P:(t % 2) * F + (k + 1) * P],
                                                   yT[:, k, t * P:(t + 1) * P], ident)
                    last.then_inc(sem("yrow_done"), 1)

            def route_rank(f):
                wait(pe, "onehot_ready", f + 1)
                width = TILES * EXPERTS
                oh = onehot[:, :, :].rearrange("p t e -> p (t e)")
                mm(ps_t[:, 0:width], tri[:, :], oh, start=True, stop=False, skip_group_check=True)
                for t in range(TILES - 1):
                    lo = (t + 1) * EXPERTS
                    mm(ps_t[:, lo:width], ones[:, :], oh[:, 0:width - lo], start=False, stop=False,
                       skip_group_check=True)
                for t in range(TILES):
                    last = mm(ps_t[:, width:width + EXPERTS], ones[:, :], oh[:, t * EXPERTS:(t + 1) * EXPERTS],
                              start=False, stop=(t == TILES - 1), skip_group_check=True)
                last.then_inc(sem("rank_done"), 1)

            def chunk(it, att_on, ffn_on):
                f = it - 1
                for j in range(JT):
                    if ffn_on:
                        if j == 0:
                            route_in(f)
                        shared_in(f, j)
                        if j == 1:
                            route_rank(f)
                        if j >= 1:
                            shared_out(f, j - 1)
                    if att_on:
                        if 1 <= j <= TILES:
                            gram(it, j - 1, ffn_on)
                        if 2 <= j <= TILES + 1:
                            attend(it, j - 2)
                        if 3 <= j <= TILES + 2:
                            turn(it, j - 3)
                        if j < TILES:
                            project(it, j)
                if att_on:
                    out_linear(it)
                if ffn_on:
                    shared_out(f, JT - 1)

            chunk(0, True, False)
            pe.wait_ge(sem("shared_in"), 64)
            pe.wait_ge(sem("weights_hi"), 2 * SPLITS)
            pe.wait_ge(sem("weights_lo"), 2 * SPLITS)
            chunk(1, True, True)
            with pe.Fori(2, NCHUNK) as it:
                chunk(it, True, True)
            chunk(NCHUNK, False, True)

            pe.wait_ge(sem("expert_in"), 16 * (2 * EXPERTS - LATE_GU - LATE_DOWN + 2))
            pe.wait_ge(sem("list_ready"), 2)
            pe.wait_ge(sem("base_ready"), NCHUNK)
            pe.wait_ge(sem("ys_ready"), TILES * NCHUNK)
            gu_flat = e_gu[:, :, :, :].rearrange("p e k f -> p (e k f)")
            dn_flat = e_down[:, :, :, :].rearrange("p e k f -> p (e k f)")

            def routed(g, u, first_body, last_body):
                i = UNROLL * g + u
                if not (last_body and u == UNROLL - 1):
                    n = u + 1
                    wait(pe, f"gat_in{n % UNROLL}", 16 * (g + 1 + n // UNROLL))
                    wait(pe, "rxT_ready", i)
                    for k in range(KT):
                        last = nc.tensor.transpose(bank[n % 2][:, k * P:(k + 1) * P],
                                                   gat[:, n % UNROLL, k * P:(k + 1) * P], ident)
                    last.then_inc(sem("rx_done"), 1)
                at = pe.value_load(woff[0:1, bass.ds(i, 1)], min_val=0, max_val=(EXPERTS - 1) * KT * F)
                wait(pe, "rxT_ready", i + 1)
                wait(pe, "rhid_ready", i - 1)
                for k in range(KT):
                    last = mm(bank[2 + u % 2][:, :], rxT[:, u % 2, k * P:(k + 1) * P],
                              gu_flat[:, bass.ds(at * 2 + k * 2 * EF, 2 * EF)], start=(k == 0), stop=(k == KT - 1))
                last.then_inc(sem("rgu_done"), 1)
                if not (first_body and u < 2):
                    routed_down(i - 2, u)
                if not (first_body and u < 1):
                    routed_turn(i - 1, u - 1)

            def routed_down(i, u):
                at = pe.value_load(woff[0:1, bass.ds(i, 1)], min_val=0, max_val=(EXPERTS - 1) * KT * F)
                wait(pe, "rhT_ready", i + 1)
                wait(pe, "res_ready", i - 1)
                for k in range(KT):
                    last = mm(bank[4 + u % 2][:, 0:F], rhT[:, u % 2, k * P:(k + 1) * P],
                              dn_flat[:, bass.ds(at + k * F, F)], start=(k == 0), stop=(k == KT - 1))
                last.then_inc(sem("rdown_done"), 1)

            def routed_turn(i, u):
                wait(pe, "rhid_ready", i + 1)
                wait(pe, "rhT_ready", i - 1)
                for k in range(KT):
                    last = nc.tensor.transpose(bank[6 + u % 2][:, k * P:(k + 1) * P],
                                               rhid[:, u % 2, k * P:(k + 1) * P], ident)
                last.then_inc(sem("rh_done"), 1)

            pe.wait_ge(sem("gat_in0"), 16)
            for k in range(KT):
                last = nc.tensor.transpose(bank[0][:, k * P:(k + 1) * P], gat[:, 0, k * P:(k + 1) * P], ident)
            last.then_inc(sem("rx_done"), 1)
            for u in range(UNROLL):
                routed(0, u, True, False)
            with pe.Fori(1, ROUTED // UNROLL - 1) as g:
                for u in range(UNROLL):
                    routed(g, u, False, False)
            for u in range(UNROLL):
                routed(ROUTED // UNROLL - 1, u, False, True)
            routed_down(ROUTED - 2, 0)
            routed_turn(ROUTED - 1, 1)
            routed_down(ROUTED - 1, 1)

        @block.scalar
        def _(act):
            dk = sc[0:BATCH, :, :].rearrange("p a b -> p (a b)")
            act.wait_ge(sem("sumsq_eps"), 1)
            nc.scalar.activation(dk[:, F:2 * F], dk[:, 0:F], ACT.Sqrt).then_inc(sem("sqrt_k"), 1)
            act.wait_ge(sem("sumsq_eps"), 2)
            nc.scalar.activation(aT[:, 1, 0:KT * BATCH], aT[:, 0, 0:KT * BATCH], ACT.Sqrt).then_inc(sem("sqrt_o"), 1)

            def aT_copy(it, t):
                wait(act, "turn_done", TILES * it + t + 1)
                if t == 0:
                    wait(act, "y_done", KT * it)
                    wait(act, "mod_ready", it + 1)
                for k in range(KT):
                    ins = nc.scalar.activation(aT[:, k, t * P:(t + 1) * P], ps_t[:, k * P:(k + 1) * P], ACT.Copy,
                                               scale=mod[:, KT + k, t // (TILES // CB):t // (TILES // CB) + 1])
                ins.then_inc(sem("aT_ready"), 1)

            def exps(it, t):
                wait(act, "s_taken", TILES * it + t + 1)
                nc.scalar.activation(sc[:, :, :], sc[:, :, :], ACT.Exp, scale=SCALE).then_inc(sem("exp_ready"), 1)

            def yT_copy(it):
                for o in range(KT):
                    wait(act, "y_done", KT * it + o + 1)
                    if o == 0:
                        wait(act, "up_done", JT * it)
                    for b in range(CB):
                        bk = (ps_k, ps_t)[o]
                        nc.scalar.activation(yT[:, o, b * SEQ:(b + 1) * SEQ], bk[:, b * SEQ:(b + 1) * SEQ],
                                             ACT.Identity, bias=biases[:, 2 * KT + o:2 * KT + o + 1],
                                             scale=mod[:, 2 * KT + o, b:b + 1]).then_inc(sem("yT_ready"), 1)
                for o in range(KT):
                    wait(act, "yT_ready", KT * CB * it + CB * (o + 1))
                    nc.scalar.activation(y_hi[:, o, :], yT[:, o, :], ACT.Copy).then_inc(sem("y_hi_ready"), 1)

            def weight_high():
                act.wait_ge(sem("shared_in"), 64)
                for n in range(SPLITS):
                    k, cols = n // (SPLITS // KT), slice(n % (SPLITS // KT) * SF * KT // SPLITS,
                                                         (n % (SPLITS // KT) + 1) * SF * KT // SPLITS)
                    for whole, hi in ((whole_gate, gate_hi), (whole_up, up_hi)):
                        nc.scalar.activation(hi[:, k, cols], whole[:, k, cols], ACT.Copy)\
                            .then_inc(sem("weights_hi"), 1)

            def silus(f, j):
                wait(act, "gate_done", JT * f + j + 1)
                wait(act, "hid_ready", JT * f + j - 1)
                nc.scalar.activation(silu[:, j % 2, :], ps_gate[:, :], ACT.Silu).then_inc(sem("silu_ready"), 1)

            def score_exp(f):
                wait(act, "top_ready", f + 1)
                nc.scalar.activation(expt[:, :], top[:, :], ACT.Exp, scale=-1.0).then_inc(sem("expt_ready"), 1)

            def ys_copy(f):
                wait(act, "score_ready", f + 1)
                wait(act, "ys_out", 16 * f)
                for t in range(TILES):
                    wait(act, "yrow_done", TILES * f + 2 * (t // 2) + 2)
                    nc.scalar.activation(ys[:, t, :], (ps_s, ps_o)[t // 2][:, (t % 2) * F:(t % 2 + 1) * F], ACT.Copy,
                                         scale=score[:, t:t + 1]).then_inc(sem("ys_ready"), 1)

            def chunk(it, att_on, ffn_on):
                f = it - 1
                for j in range(JT):
                    if att_on and 4 <= j <= TILES + 3:
                        aT_copy(it, j - 4)
                    if att_on and 2 <= j <= TILES + 1:
                        exps(it, j - 2)
                    if ffn_on:
                        if j == 0:
                            score_exp(f)
                        if j == 1:
                            ys_copy(f)
                        silus(f, j)
                if att_on:
                    yT_copy(it)

            weight_high()
            chunk(0, True, False)
            act.wait_ge(sem("filled"), 48)
            chunk(1, True, True)
            with act.Fori(2, NCHUNK) as it:
                chunk(it, True, True)
            chunk(NCHUNK, False, True)

            def rxT_copy(i, u):
                wait(act, "rx_done", i + 1)
                wait(act, "rgu_done", i - 1)
                nc.scalar.activation(rxT[:, u % 2, :], bank[u % 2][:, 0:KT * P], ACT.Copy)\
                    .then_inc(sem("rxT_ready"), 1)

            def routed(g, u, first_body, last_body):
                i = UNROLL * g + u
                if not (last_body and u == UNROLL - 1):
                    rxT_copy(i + 1, u + 1)
                wait(act, "rgu_done", i + 1)
                wait(act, "rhid_ready", i - 1)
                nc.scalar.activation(rsilu[:, u % 2, :], bank[2 + u % 2][:, 0:EF], ACT.Silu)\
                    .then_inc(sem("rsilu_ready"), 1)
                if not (first_body and u < 1):
                    rhT_copy(i - 1, u - 1)

            def rhT_copy(i, u):
                wait(act, "rh_done", i + 1)
                wait(act, "rdown_done", i - 1)
                nc.scalar.activation(rhT[:, u % 2, :], bank[6 + u % 2][:, 0:KT * P], ACT.Copy)\
                    .then_inc(sem("rhT_ready"), 1)

            rxT_copy(0, 0)
            for u in range(UNROLL):
                routed(0, u, True, False)
            with act.Fori(1, ROUTED // UNROLL - 1) as g:
                for u in range(UNROLL):
                    routed(g, u, False, False)
            for u in range(UNROLL):
                routed(ROUTED // UNROLL - 1, u, False, True)
            rhT_copy(ROUTED - 1, 1)

        @block.vector
        def _(dve):
            v = nc.vector
            dve.wait_ge(sem("consts_in"), 16)
            v.tensor_copy(tri[:, :], cst[:, C_TRI:C_TRI + P]).then_inc(sem("tri_ready"), 1)
            v.tensor_copy(count[:, :], cst[:, C_BASE:C_BASE + EXPERTS]).then_inc(sem("count_ready"), 1)
            v.tensor_copy(tokid[:, :], cst[:, C_TOK:C_TOK + TILES]).then_inc(sem("tokid_ready"), 1)
            dve.wait_ge(sem("style_done"), 1)
            dve.wait_ge(sem("bias_in"), 32)
            for w in range(2 * KT):
                v.tensor_scalar(mods[:, :, w, :], ps_k[:, w * BATCH:(w + 1) * BATCH]
                                .rearrange("p (c b) -> p c b", b=CB), biases[:, w:w + 1], None, ALU.add)\
                    .then_inc(sem("styles_ready"), 1)
            dve.wait_ge(sem("styles_ready"), 2 * KT)
            sq = kpad[:, :, :, :].rearrange("p h s d -> p (h s d)")[:, 0:2 * KT * BATCH]\
                .rearrange("p (w c b) -> p w c b", w=2 * KT, b=CB)
            for w in range(2 * KT):
                v.tensor_tensor(sq[:, w], mods[:, :, w, :], mods[:, :, w, :], ALU.mult)\
                    .then_inc(sem("sq_part"), 1)
            dve.wait_ge(sem("wk_in"), 32)
            dve.wait_ge(sem("sq_part"), 2 * KT)
            for n, wt in enumerate((wk, wo)):
                flat = wt[:, :, :].rearrange("p k o -> p (k o)")
                v.tensor_tensor(keyT[:, n, :], flat, flat, ALU.mult).then_inc(sem("squares_ready"), 1)
            dk = sc[0:BATCH, :, :].rearrange("p a b -> p (a b)")
            tmp = probT[0:BATCH, 0, :]
            do_ = aT[:, 0, 0:KT * BATCH]
            so_ = aT[:, 1, 0:KT * BATCH]
            tmo = probT[:, 1, 0:KT * BATCH]
            dve.wait_ge(sem("sumsq_done"), 2)
            v.tensor_scalar(dk[:, 0:F], ps_s[0:BATCH, 0:F], EPS, None, ALU.add).then_inc(sem("sumsq_eps"), 1)
            v.tensor_scalar(do_, ps_o[:, 0:KT * BATCH], EPS, None, ALU.add).then_inc(sem("sumsq_eps"), 1)

            def newton(name, ready, total, root, t, dest):
                dve.wait_ge(sem(ready), 1)
                w_ = t.shape[-1] // 2
                a, b = t[:, 0:w_], t[:, w_:2 * w_]
                v.reciprocal(a, root).then_inc(sem(name), 1)
                dve.wait_ge(sem(name), 1)
                v.tensor_tensor(b, a, a, ALU.mult).then_inc(sem(name), 1)
                dve.wait_ge(sem(name), 2)
                v.tensor_tensor(b, b, total, ALU.mult).then_inc(sem(name), 1)
                dve.wait_ge(sem(name), 3)
                v.tensor_scalar(b, b, -0.5, 1.5, ALU.mult, ALU.add).then_inc(sem(name), 1)
                dve.wait_ge(sem(name), 4)
                return v.tensor_tensor(dest, a if len(dest.shape) == 2 else a.rearrange("p (c b) -> p c b", b=CB),
                                       b if len(dest.shape) == 2 else b.rearrange("p (c b) -> p c b", b=CB), ALU.mult)

            newton("newton_k", "sqrt_k", dk[:, 0:F], dk[:, F:2 * F], tmp, dk[:, F:2 * F]).then_inc(sem("demod_k"), 1)
            for o in range(KT):
                cols = slice(o * BATCH, (o + 1) * BATCH)
                newton(f"newton_o{o}", "sqrt_o", do_[:, cols], so_[:, cols],
                       probT[:, 1, 2 * o * BATCH:2 * (o + 1) * BATCH], mods[:, :, 2 * KT + o, :])\
                    .then_inc(sem("mods_ready"), 1)
            v.memset(ps_s[:, :], 0.0).then_inc(sem("banks_set"), 1)
            v.memset(ps_o[:, :], 0.0).then_inc(sem("banks_set"), 1)
            for s in range(2):
                v.tensor_scalar(bias_kp[:, s, :], bias_k[:, :], parity[:, s:s + 1], None, ALU.mult)\
                    .then_inc(sem("bias_ready"), 1)
            dve.wait_ge(sem("bias_ready"), 2)
            dve.wait_ge(sem("mods_ready"), KT)
            dve.wait_ge(sem("ones_ready"), 1)
            dve.wait_ge(sem("demod_out"), 16)

            def modulate(it):
                wait(dve, "yT_ready", KT * CB * it)
                wait(dve, "wkb_ready", it)
                v.tensor_copy(mod[:, :, :], mods[:, bass.ds(it, 1), :, :].rearrange("p c w b -> p (c w) b"))\
                    .then_inc(sem("mod_ready"), 1)
                wait(dve, "mod_ready", it + 1)
                wait(dve, "demod_in", 16 * (it + 1))
                wait(dve, "proj_done", TILES * it)
                for b in range(CB):
                    for k in range(KT):
                        ins = v.scalar_tensor_tensor(wkb[:, b, k, :], wk[:, k, :], mod[:, k, b:b + 1],
                                                     demod_b[:, b, :], ALU.mult, ALU.mult)
                ins.then_inc(sem("wkb_ready"), 1)

            def keys(it, t):
                wait(dve, "proj_done", TILES * it + t + 1)
                wait(dve, "keyT_ready", TILES * it + t)
                for s in range(2):
                    v.scalar_tensor_tensor(kpad[:, :, s, :], ps_k[:, 0:F].rearrange("p (h d) -> p h d", h=HEADS),
                                           parity[:, s:s + 1],
                                           bias_kp[:, s, :].rearrange("p (h d) -> p h d", h=HEADS),
                                           ALU.mult, ALU.add).then_inc(sem("k_taken"), 1)
                wait(dve, "k_taken", 2 * (TILES * it + t + 1))
                wait(dve, "gram_done", TILES * it + t - 1)
                wait(dve, "val_ready", TILES * it + t - 1)
                v.transpose(keyT[:, t % 2, :].rearrange("p (t h) -> p h t", h=HEADS),
                            kpad[:, :, :, :].rearrange("p h s d -> p h (s d)")).then_inc(sem("keyT_ready"), 1)
                wait(dve, "keyT_ready", TILES * it + t + 1)
                pairs = keyT[:, t % 2, :].rearrange("p (r s h) -> p r s h", s=2, h=HEADS)
                v.tensor_tensor(keysum[:, t % 2, :].rearrange("p (r h) -> p r h", h=HEADS), pairs[:, :, 0, :],
                                pairs[:, :, 1, :], ALU.add).then_inc(sem("keysum_ready"), 1)
                wait(dve, "av_done", TILES * it + t - 1)
                v.transpose(val[:, t % 2, :], keyT[:, t % 2, :]).then_inc(sem("val_ready"), 1)

            def soft(it, t):
                wait(dve, "gram_done", TILES * it + t + 1)
                wait(dve, "s_taken", TILES * it + t)
                scores = ps_s[:, :].rearrange("p (a b) -> p a b", b=HEADS)
                v.tensor_reduce(rowmax[:, :], scores, AX.X, ALU.max).then_inc(sem("max_ready"), 1)
                wait(dve, "max_ready", TILES * it + t + 1)
                wait(dve, "probT_ready", TILES * it + t)
                v.tensor_tensor(sc[:, :, :], scores, rowmax[:, :].unsqueeze(2).to_broadcast([P, 32, HEADS]),
                                ALU.subtract).then_inc(sem("s_taken"), 1)

            def soft_turn(it, t):
                wait(dve, "exp_ready", TILES * it + t + 1)
                wait(dve, "av_done", TILES * it + t - 1)
                v.transpose(probT[:, t % 2, :], sc[:, :, :].rearrange("p a b -> p (a b)"))\
                    .then_inc(sem("probT_ready"), 1)
                v.tensor_reduce(z[:, :], sc[:, :, :], AX.X, ALU.add).then_inc(sem("z_ready"), 1)
                wait(dve, "z_ready", TILES * it + t + 1)
                v.transpose(zT[:, :], z[:, :]).then_inc(sem("zT_ready"), 1)
                wait(dve, "zT_ready", TILES * it + t + 1)
                v.reciprocal(rz[:, t % 2, :], zT[:, 0:HEADS]).then_inc(sem("rz_ready"), 1)

            def normalise(it, t):
                wait(dve, "av_done", TILES * it + t + 1)
                wait(dve, "att_ready", TILES * it + t)
                v.transpose(ot[:, :, :], ps_o[:, :].rearrange("p (t d) -> p d t", d=D)).then_inc(sem("o_taken"), 1)
                wait(dve, "o_taken", TILES * it + t + 1)
                wait(dve, "rz_ready", TILES * it + t + 1)
                wait(dve, "turn_done", TILES * it + t)
                v.tensor_tensor(att[:, :].rearrange("p (h d) -> p h d", h=HEADS),
                                ot[:, :, 0:HEADS].rearrange("p d h -> p h d"),
                                rz[:, t % 2, :].unsqueeze(2).to_broadcast([P, HEADS, D]), ALU.mult)\
                    .then_inc(sem("att_ready"), 1)

            def split_y(f):
                for o in range(KT):
                    wait(dve, "y_hi_ready", KT * f + o + 1)
                    v.tensor_tensor(y_lo[:, o, :], yT[:, o, :], y_hi[:, o, :].bitcast(F32), ALU.subtract)\
                        .then_inc(sem("y_lo_ready"), 1)

            def weight_low(n):
                dve.wait_ge(sem("weights_hi"), 2 * (n + 1))
                k, cols = n // (SPLITS // KT), slice(n % (SPLITS // KT) * SF * KT // SPLITS,
                                                     (n % (SPLITS // KT) + 1) * SF * KT // SPLITS)
                for whole, hi, lo in ((whole_gate, gate_hi, gate_lo), (whole_up, up_hi, up_lo)):
                    v.tensor_tensor(lo[:, k, cols], whole[:, k, cols], hi[:, k, cols].bitcast(F32), ALU.subtract)\
                        .then_inc(sem("weights_lo"), 1)

            def hidden(f, j):
                wait(dve, "up_done", JT * f + j + 1)
                wait(dve, "silu_ready", JT * f + j + 1)
                wait(dve, "down_done", JT * f + j - 1)
                v.tensor_tensor(hid[:, j % 2, :], ps_up[:, :], silu[:, j % 2, :], ALU.mult)\
                    .then_inc(sem("hid_ready"), 1)

            def per_tile(a):
                return a.unsqueeze(2).to_broadcast([P, TILES, EXPERTS])

            def per_expert(a):
                return a.unsqueeze(1).to_broadcast([P, TILES, EXPERTS])

            def choose(f):
                logits = ps_t[:, 0:TILES * EXPERTS].rearrange("p (t e) -> p t e", e=EXPERTS)
                wait(dve, "logit_done", f + 1)
                wait(dve, "score_ready", f)
                wait(dve, "slot_ready", f)
                v.tensor_reduce(top[:, :], logits, AX.X, ALU.max).then_inc(sem("top_ready"), 1)
                wait(dve, "top_ready", f + 1)
                v.tensor_tensor(eq[:, :, :], logits, per_tile(top[:, :]), ALU.is_equal).then_inc(sem("eq_ready"), 1)
                wait(dve, "eq_ready", f + 1)
                v.tensor_tensor(pick[:, :, :], eq[:, :, :], per_expert(erev), ALU.mult).then_inc(sem("pick_ready"), 1)
                wait(dve, "pick_ready", f + 1)
                v.tensor_reduce(pickmax[:, :], pick[:, :, :], AX.X, ALU.max).then_inc(sem("pickmax_ready"), 1)
                wait(dve, "pickmax_ready", f + 1)
                v.tensor_tensor(onehot[:, :, :], pick[:, :, :], per_tile(pickmax[:, :]), ALU.is_equal)\
                    .then_inc(sem("onehot_ready"), 1)

            def score_of(f):
                wait(dve, "expt_ready", f + 1)
                wait(dve, "ys_ready", TILES * f)
                v.tensor_scalar(ex1[:, :], expt[:, :], 1.0, None, ALU.add).then_inc(sem("ex1_ready"), 1)
                wait(dve, "ex1_ready", f + 1)
                v.reciprocal(score[:, :], ex1[:, :]).then_inc(sem("score_ready"), 1)

            def place(f, first_chunk):
                width = TILES * EXPERTS
                wait(dve, "rank_done", f + 1)
                wait(dve, "count_ready", f + 1)
                v.tensor_tensor(rank[:, :, :], ps_t[:, 0:width].rearrange("p (t e) -> p t e", e=EXPERTS),
                                per_expert(count[:, :]), ALU.add).then_inc(sem("rank_ready"), 1)
                wait(dve, "rank_ready", f + 1)
                v.tensor_tensor(count[:, :], count[:, :], ps_t[:, width:width + EXPERTS], ALU.add)\
                    .then_inc(sem("count_ready"), 1)
                wait(dve, "count_ready", f + 2)
                v.tensor_tensor(slotsel[:, :, :], rank[:, :, :], onehot[:, :, :], ALU.mult)\
                    .then_inc(sem("rank_taken"), 1)
                wait(dve, "rank_taken", f + 1)
                v.tensor_reduce(slotf[:, :], slotsel[:, :, :], AX.X, ALU.add).then_inc(sem("slotf_ready"), 1)
                wait(dve, "slotf_ready", f + 1)
                if not first_chunk:
                    wait(dve, "slots_out", 16 * TILES * f)
                    wait(dve, "tokid_ready", f)
                    v.tensor_scalar(tokid[:, :], tokid[:, :], float(CHUNK), None, ALU.add)\
                        .then_inc(sem("tokid_ready"), 1)
                wait(dve, "tokid_ready", f + 1)
                v.tensor_copy(slot[:, :], slotf[:, :]).then_inc(sem("slot_ready"), 1)

            def sum_rows(f):
                wait(dve, "down_done", JT * (f + 1))
                wait(dve, "residual_in", 16 * (f + 1))
                for n, bk in enumerate((ps_sh0, ps_sh1)):
                    ins = v.tensor_tensor(base[:, 2 * n:2 * n + 2, :], bk[:, :].rearrange("p (t f) -> p t f", f=F),
                                          base[:, 2 * n:2 * n + 2, :], ALU.add)
                ins.then_inc(sem("base_ready"), 1)

            def chunk(it, att_on, ffn_on, first_ffn=False):
                f = it - 1
                if ffn_on:
                    split_y(f)
                if att_on:
                    modulate(it)
                for j in range(JT):
                    if ffn_on and j == 0:
                        choose(f)
                        score_of(f)
                    if not ffn_on and j >= JT - SPLITS:
                        weight_low(j - JT + SPLITS)
                    if att_on:
                        if 2 <= j <= TILES + 1:
                            soft(it, j - 2)
                        if 1 <= j <= TILES:
                            keys(it, j - 1)
                    if ffn_on and j == 1:
                        place(f, first_ffn)
                    if att_on:
                        if 2 <= j <= TILES + 1:
                            soft_turn(it, j - 2)
                        if 3 <= j <= TILES + 2:
                            normalise(it, j - 3)
                    if ffn_on:
                        hidden(f, j)
                if ffn_on:
                    sum_rows(f)

            chunk(0, True, False)
            dve.wait_ge(sem("filled"), 48)
            chunk(1, True, True, True)
            with dve.Fori(2, NCHUNK) as it:
                chunk(it, True, True)
            chunk(NCHUNK, False, True)

            step = [0]

            def link(ins):
                step[0] += 1
                ins.then_inc(sem("list_step"), 1)
                dve.wait_ge(sem("list_step"), step[0])

            dve.wait_ge(sem("count_ready"), NCHUNK + 1)
            NK = TOKENS // P
            link(v.tensor_tensor(held[:, :], count[0:1, :], cst[0:1, C_BASE:C_BASE + EXPERTS], ALU.subtract))
            link(v.tensor_tensor(more[:, :, :], held[:, :].unsqueeze(2).to_broadcast([1, EXPERTS, NK]),
                                 cst[0:1, C_STEP:C_STEP + NK].unsqueeze(1).to_broadcast([1, EXPERTS, NK]), ALU.is_gt))
            link(v.tensor_reduce(ntile[:, :], more[:, :, :], AX.X, ALU.add))
            link(v.memset(held[:, :], 1.0))
            link(v.tensor_tensor_scan(tend[:, :], held[:, :], ntile[:, :], 0.0, ALU.mult, ALU.add))
            numbers = cst[0:1, C_TILE:C_TILE + ROUTED]
            link(v.tensor_tensor(before[:, :, :], tend[:, :].unsqueeze(1).to_broadcast([1, ROUTED, EXPERTS]),
                                 numbers.unsqueeze(2).to_broadcast([1, ROUTED, EXPERTS]), ALU.is_le))
            link(v.tensor_reduce(which[:, :], before[:, :, :], AX.X, ALU.add))
            link(v.tensor_tensor(weighed[:, :, :], before[:, :, :],
                                 ntile[:, :].unsqueeze(1).to_broadcast([1, ROUTED, EXPERTS]), ALU.mult))
            link(v.tensor_reduce(first[:, :], weighed[:, :, :], AX.X, ALU.add))
            link(v.tensor_tensor(within[:, :], numbers, first[:, :], ALU.subtract))
            link(v.tensor_scalar(within[:, :], within[:, :], float(P), None, ALU.mult))
            link(v.scalar_tensor_tensor(offf[:, :], which[:, :], float(TOKENS), within[:, :], ALU.mult, ALU.add))
            v.tensor_copy(off[:, :], offf[:, :]).then_inc(sem("list_ready"), 1)
            link(v.tensor_scalar(wofff[:, :], which[:, :], float(EXPERTS - 1), float(KT * F), ALU.min, ALU.mult))
            v.tensor_copy(woff[:, :], wofff[:, :]).then_inc(sem("list_ready"), 1)

            def rhidden(g, u, first_body):
                i = UNROLL * g + u
                wait(dve, "rgu_done", i + 1)
                wait(dve, "rsilu_ready", i + 1)
                wait(dve, "rh_done", i - 1)
                v.tensor_tensor(rhid[:, u % 2, :], bank[2 + u % 2][:, EF:2 * EF], rsilu[:, u % 2, :], ALU.mult)\
                    .then_inc(sem("rhid_ready"), 1)
                if not (first_body and u < 2):
                    result(i - 2, u - 2, g if u >= 2 else g - 1)

            def result(i, u, g):
                wait(dve, "rdown_done", i + 1)
                wait(dve, f"res_out{u % UNROLL}", 16 * g)
                v.tensor_tensor(res[:, u % UNROLL, :], bank[4 + u % 2][:, 0:F], gat[:, u % UNROLL, F:2 * F], ALU.add)\
                    .then_inc(sem("res_ready"), 1)

            for u in range(UNROLL):
                rhidden(0, u, True)
            with dve.Fori(1, ROUTED // UNROLL) as g:
                for u in range(UNROLL):
                    rhidden(g, u, False)
            for u in (UNROLL - 2, UNROLL - 1):
                result(ROUTED - UNROLL + u, u, ROUTED // UNROLL - 1)


NAMES = ["xT", "x", "condT", "k_affT", "k_wT", "k_b", "o_affT", "o_wT", "bias_cols", "routerT",
         "gate_up", "down", "sh_gateT", "sh_upT", "sh_downT", "consts"]


def constants(np):
    c = np.zeros((P, C_END), np.float32)
    i = np.arange(P)
    c[:, C_ID:C_ID + P] = np.eye(P)
    c[:, C_TRI:C_TRI + P] = i[:, None] < i[None, :]
    c[:, C_PAR:C_PAR + 2] = i[:, None] % 2 == np.arange(2)[None, :]
    c[:, C_REV:C_REV + EXPERTS] = EXPERTS - np.arange(EXPERTS)
    c[:, C_BASE:C_BASE + EXPERTS] = TOKENS * np.arange(EXPERTS)
    c[:, C_STEP:C_STEP + TOKENS // P] = P * np.arange(TOKENS // P)
    c[:, C_TILE:C_TILE + ROUTED] = np.arange(ROUTED)
    c[:, C_TOK:C_TOK + TILES] = i[:, None] + P * np.arange(TILES)[None, :]
    return c


def kernel(x, cond_512, L0_cond_k_aff_w, L0_cond_k_aff_b, L0_cond_k_w, L0_cond_k_b, L0_cond_o_aff_w,
           L0_cond_o_aff_b, L0_cond_o_w, L0_cond_o_b, L0_ffn_router_w, L0_ffn_gate_up_proj, L0_ffn_down_proj,
           L0_ffn_shared_gate_w, L0_ffn_shared_up_w, L0_ffn_shared_down_w):
    import numpy as np
    import concourse.bacc as bacc
    from concourse.bass_utils import run_bass_kernel_spmd

    flat = np.ascontiguousarray(x).reshape(TOKENS, F)
    data = dict(
        xT=flat.reshape(NCHUNK, CHUNK, KT, P).transpose(0, 3, 2, 1),
        x=flat.reshape(TOKENS // P, P, F),
        condT=np.asarray(cond_512).T,
        k_affT=np.asarray(L0_cond_k_aff_w).T, k_wT=np.asarray(L0_cond_k_w).T, k_b=L0_cond_k_b,
        o_affT=np.asarray(L0_cond_o_aff_w).T, o_wT=np.asarray(L0_cond_o_w).T,
        bias_cols=np.stack([np.asarray(b).reshape(KT, P).T
                            for b in (L0_cond_k_aff_b, L0_cond_o_aff_b, L0_cond_o_b)], axis=1).reshape(P, 3 * KT),
        routerT=np.asarray(L0_ffn_router_w).T, gate_up=L0_ffn_gate_up_proj, down=L0_ffn_down_proj,
        sh_gateT=np.asarray(L0_ffn_shared_gate_w).T, sh_upT=np.asarray(L0_ffn_shared_up_w).T,
        sh_downT=np.asarray(L0_ffn_shared_down_w).T, consts=constants(np),
    )
    nc = bacc.Bacc("TRN2", target_bir_lowering=False, num_devices=1)
    arrays, args = {}, []
    for name in NAMES:
        a = np.ascontiguousarray(data[name])
        arrays["in_" + name] = a
        args.append(nc.dram_tensor("in_" + name, a.shape, mybir.dt.from_np(a.dtype), kind="ExternalInput").ap())
    out = nc.dram_tensor("out_rows", (TOKENS, F), F32, kind="ExternalOutput").ap()
    build_program(nc, *args, out)
    r = run_bass_kernel_spmd(nc, [arrays], core_ids=[0])
    return r.results[0]["out_rows"].reshape(BATCH, SEQ, F)
```

```python
from contextlib import ExitStack

import concourse.bass as bass
from concourse import mybir

F32 = mybir.dt.float32
F32R = mybir.dt.float32r
BF16 = mybir.dt.bfloat16
I32 = mybir.dt.int32
ALU = mybir.AluOpType
ACT = mybir.ActivationFunctionType
AX = mybir.AxisListType

P = 128
BATCH, SEQ, F = 32, 256, 256
HEADS, D = 16, 16
EXPERTS, EF = 16, 256
SF = 1024
TOKENS = BATCH * SEQ
KT = F // P
CHUNK = 512
TILES = CHUNK // P
CB = CHUNK // SEQ
NCHUNK = TOKENS // CHUNK
Q = 4
PAIRS = 16
JT = SF // P
NMOD = 6
ROUTED = TOKENS // P + EXPERTS
LEAD = 7
SPLITS = 4
UNROLL = 10
TABLE = EXPERTS * TOKENS + ROUTED * P
EMPTY = TOKENS
UP_FIRST = 3
LATE_GU = 2
LATE_DOWN = 5
EXPERTS_IN = 16 * (2 * EXPERTS + 1)
EPS = 1e-8
SCALE = 1.0 / D ** 0.5

C_ID = 0
C_TRI = C_ID + P
C_PAR = C_TRI + P
C_REV = C_PAR + 2
C_BASE = C_REV + EXPERTS
C_STEP = C_BASE + EXPERTS
C_TILE = C_STEP + TOKENS // P
C_TOK = C_TILE + ROUTED
C_END = C_TOK + TILES
ARENA = UNROLL * 2 * F + 6 * F + UNROLL * F


def build_program(nc, xT, x, condT, k_affT, k_wT, k_b, o_affT, o_wT, bias_cols, routerT,
                  gate_up, down, sh_gateT, sh_upT, sh_downT, consts, out):
    demod_rows = nc.dram_tensor("demod_rows", [BATCH, F], F32).ap()
    slot_table = nc.dram_tensor("slot_table", [TABLE, 1], I32).ap()
    y_rows = nc.dram_tensor("y_rows", [TOKENS + 1, F], F32).ap()
    rows = nc.dram_tensor("routed_rows", [TOKENS + 1, 2 * F], F32).ap()

    ctx = ExitStack()
    with ctx:
        def sb(name, shape, dt=F32):
            return ctx.enter_context(nc.sbuf_tensor("sb_" + name, shape, dt))

        made = {}
        passed = {nc.sync: "loads_passed", nc.gpsimd: "indirect_passed"}

        def sem(name):
            if name not in made:
                made[name] = ctx.enter_context(nc.semaphore(name))
            return made[name]

        def wait(eng, name, n):
            if not isinstance(n, int) or n > 0:
                eng.wait_ge(sem(name), n)
            if not isinstance(n, int) and eng in passed:
                eng.sem_inc(sem(passed[eng]), 1)

        cst = sb("consts", [P, C_END])
        tri = sb("tri", [P, P], BF16)
        ones = sb("ones", [P, P], BF16)
        wk = sb("wk", [P, KT, F])
        wo_hi = sb("wo_hi", [P, KT, F], F32R)
        turner = sb("turner", [P, 2 * (P + EXPERTS)])
        gate_hi = sb("gate_hi", [P, JT, KT, P], F32R)
        up_hi = sb("up_hi", [P, JT, KT, P], F32R)
        down_hi = sb("down_hi", [P, JT, F], F32R)
        down_lo = sb("down_lo", [P, JT, F], F32R)
        gu_base = -(-nc.sbuf_base // 32) * 32
        e_gu = sb("e_gu", [P, EXPERTS, KT, 2 * EF])
        down_base = -(-nc.sbuf_base // 32) * 32
        e_down = sb("e_down", [P, EXPERTS, KT, F])
        gate_lo = nc.alloc_sbuf_tensor_at("sb_gate_lo", [P, JT, KT, P], F32R,
                                          offset=gu_base + (EXPERTS - LATE_GU) * KT * 2 * EF * 4)
        up_lo = nc.alloc_sbuf_tensor_at("sb_up_lo", [P, JT, KT, P], F32R,
                                        offset=down_base + (EXPERTS - LATE_DOWN + 1) * KT * F * 4)
        wo_lo = nc.alloc_sbuf_tensor_at("sb_wo_lo", [P, KT, F], F32R,
                                        offset=down_base + (EXPERTS - LATE_DOWN) * KT * F * 4)
        bias_k = sb("bias_k", [P, F])
        bias_kp = sb("bias_kp", [P, 2, F])
        biases = sb("biases", [P, 3 * KT])
        mods = sb("mods", [P, NCHUNK, NMOD, CB])
        mod = sb("mod", [P, NMOD, CB])
        arena_base = -(-nc.sbuf_base // 32) * 32
        arena = sb("arena", [P, ARENA])
        taken = [0]

        def part(*shape):
            n = 1
            for m in shape:
                n *= m
            lo = taken[0]
            taken[0] += n
            ap = arena[:, lo:lo + n]
            names = "abc"[:len(shape)]
            if len(shape) > 1:
                ap = ap.rearrange(f"p ({' '.join(names)}) -> p {' '.join(names)}", **dict(zip(names[1:], shape[1:])))
            return ap

        xt = part(KT, CHUNK)
        wkb = part(CB, KT, F)
        kpad = part(HEADS, 2, D)
        keyT = part(32 * HEADS)
        val = part(2, PAIRS * 32)
        keysum = part(PAIRS * HEADS)
        sc = part(32, HEADS)
        probT = part(2, PAIRS * 32)
        ot = part(D, 32)
        att = part(HEADS * D)
        hid = part(CHUNK)

        def parts_of(name, *shape):
            n = shape[0] * shape[1]
            at = nc.alloc_sbuf_tensor_at("sb_" + name, [P, *shape], F32R, offset=arena_base + 4 * taken[0])
            taken[0] += n
            assert taken[0] <= ARENA
            return at

        aT_hi = parts_of("aT_hi", KT, CHUNK)
        aT_lo = parts_of("aT_lo", KT, CHUNK)
        demod_b = sb("demod_b", [P, CB, F])
        rowmax = sb("rowmax", [P, 32])
        z = sb("z", [P, 32])
        zT = sb("zT", [P, 32])
        rz = sb("rz", [P, 2, HEADS])
        yT = sb("yT", [P, KT, CHUNK])
        y_hi = sb("y_hi", [P, KT, CHUNK], F32R)
        y_lo = sb("y_lo", [P, KT, CHUNK], F32R)
        silu = sb("silu", [P, CHUNK])
        hid_hi = sb("hid_hi", [P, CHUNK], F32R)
        hid_lo = sb("hid_lo", [P, CHUNK], F32R)
        base = sb("base", [P, TILES, F])
        ys = sb("ys", [P, TILES, F])
        sharedT = ys[:, :, :].rearrange("p t f -> p (t f)").rearrange("p (k t) -> p k t", k=KT)
        top = sb("top", [P, TILES])
        expt = sb("expt", [P, TILES])
        ex1 = sb("ex1", [P, TILES])
        score = sb("score", [P, TILES])
        eq = sb("eq", [P, TILES, EXPERTS])
        pick = sb("pick", [P, TILES, EXPERTS])
        pickmax = sb("pickmax", [P, TILES])
        onehot = sb("onehot", [P, TILES, EXPERTS], BF16)
        rank = sb("rank", [P, TILES, EXPERTS])
        slotsel = sb("slotsel", [P, TILES, EXPERTS])
        slotf = sb("slotf", [P, TILES])
        slot = sb("slot", [P, TILES], I32)
        tokid = sb("tokid", [P, TILES], I32)
        count = sb("count", [P, EXPERTS])
        held = sb("held", [1, EXPERTS])
        ntile = sb("ntile", [1, EXPERTS])
        tend = sb("tend", [1, EXPERTS])
        which = sb("which", [1, ROUTED])
        first = sb("first", [1, ROUTED])
        within = sb("within", [1, ROUTED])
        offf = sb("offf", [1, ROUTED])
        wofff = sb("wofff", [1, ROUTED])
        off = sb("off", [1, ROUTED], I32)
        woff = sb("woff", [1, ROUTED], I32)
        idx = sb("idx", [P, UNROLL], I32)
        idx_half = sb("idx_half", [P, LEAD], I32)
        taken[0] = 0
        gat = part(UNROLL, 2 * F)
        rsilu = part(2, EF)
        rhid = part(2, EF)
        rhT = part(2, KT * P)
        res = part(UNROLL, F)
        rx_hi, rx_lo = (w[:, :, :].rearrange("p k (u t) -> p (k u) t", t=KT * P) for w in (y_hi, y_lo))
        gu_hi, gu_lo = (w[:, :, :, :].rearrange("p (u j) k o -> p u (j k o)", u=2) for w in (gate_hi, up_hi))
        taken[0] = 0
        more = part(EXPERTS, TOKENS // P)[0:1]
        before = part(ROUTED, EXPERTS)[0:1]
        weighed = part(ROUTED, EXPERTS)[0:1]

        bank = [ctx.enter_context(nc.psum_tensor(f"bank{i}", [P, 512], F32)) for i in range(8)]
        ps_gate, ps_up, ps_sh0, ps_sh1, ps_k, ps_s, ps_o, ps_t = bank
        row_banks = (ps_s, ps_o, ps_t, ps_sh1)
        HALF = P + EXPERTS
        ident = cst[:, C_ID:C_ID + P]
        erev = cst[:, C_REV:C_REV + EXPERTS]
        parity = cst[:, C_PAR:C_PAR + 2]

        whole_gate, whole_up = (e_gu[:, 10 + 2 * n:12 + 2 * n, :, :].rearrange("p e k f -> p (e k f)")
                                .rearrange("p (k j o) -> p k j o", k=KT, j=JT) for n in range(2))

        whole_down = e_gu[:, 8:10, :, :].rearrange("p e k f -> p (e k f)").rearrange("p (j o) -> p j o", j=JT)
        osum = ot[:, 8:12, :].rearrange("p a b -> p (a b)").rearrange("p (n c) -> p n c", n=2)
        whole_wo = e_gu[:, 7, 0, :].rearrange("p (k o) -> p k o", k=KT)
        summed = ((1, ps_k), (0, ps_sh0))

        block = ctx.enter_context(nc.Block())

        gu_flat = e_gu[:, :, :, :].rearrange("p e k f -> p (e k f)")

        def gate_up_of(eng, i):
            at = eng.value_load(woff[0:1, bass.ds(i, 1)], min_val=0, max_val=(EXPERTS - 1) * KT * F)
            return gu_flat[:, bass.ds(at * 2, KT * 2 * EF)]

        @block.sync
        def _(sp):
            sp.dma_start(cst[:, :], consts).then_inc(sem("consts_in"), 16)
            sp.dma_start(ot[:, :, :].rearrange("p d h -> p (d h)")[:, 0:BATCH], condT)\
                .then_inc(sem("cond_in"), 16)
            sp.dma_start(att[:, 0:F], k_affT).then_inc(sem("cond_in"), 16)
            sp.dma_start(sc[:, :, :].rearrange("p a b -> p (a b)")[:, 0:F], o_affT).then_inc(sem("cond_in"), 16)
            sp.dma_start(wk[:, :, :], k_wT.rearrange("(k p) o -> p k o", p=P)).then_inc(sem("wk_in"), 16)
            sp.dma_start(whole_wo, o_wT.rearrange("(k p) o -> p k o", p=P)).then_inc(sem("wk_in"), 16)
            sp.dma_start(biases[:, :], bias_cols).then_inc(sem("bias_in"), 16)
            sp.dma_start(bias_k[:, :], k_b.partition_broadcast(P)).then_inc(sem("bias_in"), 16)
            sp.dma_start(xt[:, :, :], xT[0, :, :, :]).then_inc(sem("xt_in"), 16)
            sp.dma_start(whole_gate.rearrange("p k j o -> p k (j o)"), sh_gateT.rearrange("(k p) o -> p k o", p=P)).then_inc(sem("shared_in"), 16)
            sp.dma_start(whole_up.rearrange("p k j o -> p k (j o)"), sh_upT.rearrange("(k p) o -> p k o", p=P)).then_inc(sem("shared_in"), 16)
            sp.dma_start(whole_down, sh_downT.rearrange("(j p) o -> p j o", p=P)).then_inc(sem("shared_in"), 16)
            sp.dma_start(turner[:, P:P + KT * EXPERTS].rearrange("p (k o) -> p k o", k=KT),
                         routerT.rearrange("(k p) o -> p k o", p=P)).then_inc(sem("shared_in"), 16)
            for lo in (0, P + KT * EXPERTS):
                sp.dma_start(turner[:, lo:lo + P], consts[:, C_ID:C_ID + P]).then_inc(sem("shared_in"), 16)
            sp.wait_ge(sem("fill_ready"), 2)
            fill = ys[:, :, :].rearrange("p t f -> p (t f)").bitcast(I32)
            whole = EXPERTS * TOKENS
            sp.dma_start(slot_table[0:whole, :].rearrange("(p t) o -> p (t o)", p=P), fill)\
                .then_inc(sem("filled"), 16)
            sp.dma_start(slot_table[whole:TABLE, :].rearrange("(p t) o -> p (t o)", p=P), fill[:, 0:ROUTED])\
                .then_inc(sem("filled"), 16)
            sp.dma_start(rows[TOKENS:TOKENS + 1, :], base[0:1, 0:2, :].rearrange("p t f -> p (t f)"))\
                .then_inc(sem("filled"), 16)
            sp.dma_start(y_rows[TOKENS:TOKENS + 1, :], base[0:1, 0, :]).then_inc(sem("filled"), 16)
            sp.wait_ge(sem("demod_k"), 1)
            sp.dma_start(demod_rows, sc[0:BATCH, :, :].rearrange("p a b -> p (a b)")[:, F:2 * F])\
                .then_inc(sem("demod_out"), 16)
            sp.wait_ge(sem("demod_out"), 16)

            def load_slots(g, u):
                at = sp.value_load(off[0:1, bass.ds(UNROLL * g + u, 1)], min_val=0, max_val=TABLE - P)
                wait(sp, f"res_out{u}", 16 * g)
                sp.dma_start(idx[:, u:u + 1], slot_table[bass.ds(at, P), :]).then_inc(sem(f"idx_in{u}"), 16)

            def load_slots_first():
                sp.wait_ge(sem("list_ready"), 2)
                sp.wait_ge(sem("slots_out"), 16 * TILES * NCHUNK)
                for u in range(LEAD):
                    load_slots(0, u)

            def load_wide(lo, k0=0, k1=KT):
                sp.dma_start(e_gu[:, bass.ds(lo, 1), k0:k1, :].rearrange("p e k f -> p (e k) f"),
                             gate_up[bass.ds(lo, 1), k0 * P:k1 * P, :].rearrange("e (k p) f -> p (e k) f", p=P))\
                    .then_inc(sem("expert_in"), 16)

            def load_deep(lo):
                sp.dma_start(e_down[:, bass.ds(lo, 1), :, :].rearrange("p e k f -> p (e k) f"),
                             down[bass.ds(lo, 1), :, :].rearrange("e (k p) f -> p (e k) f", p=P))\
                    .then_inc(sem("expert_in"), 16)

            def chunk(it, att_on, ffn_on, ahead, wide=False, deep=False):
                if ffn_on:
                    wait(sp, "base_out", 16 * (it - 1))
                    sp.dma_start(base[:, :, :], x[bass.ds((it - 1) * TILES, TILES), :, :].rearrange("t p f -> p t f"))\
                        .then_inc(sem("residual_in"), 16)
                if ahead:
                    wait(sp, "wkb_ready", it + 1)
                    sp.dma_start(demod_b[:, :, :],
                                 demod_rows[bass.ds((it + 1) * CB, CB), :].partition_broadcast(P))\
                        .then_inc(sem("demod_in"), 16)
                if ffn_on:
                    wait(sp, "ys_ready", TILES * it)
                    sp.dma_start(rows[bass.ds((it - 1) * CHUNK, CHUNK), 0:F].rearrange("(t p) f -> p t f", p=P),
                                 ys[:, :, :]).then_inc(sem("ys_out"), 16)
                    sp.dma_start(y_rows[bass.ds((it - 1) * CHUNK, CHUNK), :].rearrange("(t p) f -> p t f", p=P),
                                 ys[:, :, :]).then_inc(sem("ys_out"), 16)
                if ahead:
                    wait(sp, "proj_done", TILES * (it + 1))
                    sp.dma_start(xt[:, :, :], xT[bass.ds(it + 1, 1), :, :, :].rearrange("a p k t -> p (a k) t"))\
                        .then_inc(sem("xt_in"), 16)
                if wide:
                    load_wide(it)
                if deep:
                    load_deep(it)
                if not att_on:
                    sp.wait_ge(sem("y_done"), KT * NCHUNK)
                    load_deep(EXPERTS - LATE_DOWN)
                    sp.wait_ge(sem("up_done"), JT * (NCHUNK - 1) + 4)
                    load_wide(EXPERTS - 2)
                    load_deep(EXPERTS - 4)
                    load_deep(EXPERTS - 3)
                    load_slots_first()
                    sp.wait_ge(sem("up_done"), JT * (NCHUNK - 1) + 6)
                    load_wide(EXPERTS - 1, 0, 1)
                    load_deep(EXPERTS - 2)
                    sp.wait_ge(sem("up_done"), JT * NCHUNK)
                    load_wide(EXPERTS - 1, 1, 2)
                    load_deep(EXPERTS - 1)
                if ffn_on:
                    wait(sp, "base_ready", 2 * it)
                    sp.dma_start(rows[bass.ds((it - 1) * CHUNK, CHUNK), F:2 * F].rearrange("(t p) f -> p t f", p=P),
                                 base[:, :, :]).then_inc(sem("base_out"), 16)

            chunk(0, True, False, True, True, True)
            sp.wait_ge(sem("filled"), 64)
            chunk(1, True, True, True, True, True)
            sp.wait_ge(sem("weights_lo"), 3 * SPLITS)
            sp.wait_ge(sem("wo_lo_ready"), 1)
            with sp.Fori(2, EXPERTS - LATE_DOWN) as it:
                chunk(it, True, True, True, True, True)
            for it in range(EXPERTS - LATE_DOWN, NCHUNK):
                chunk(it, True, True, it < NCHUNK - 1, it < EXPERTS - LATE_GU, False)
            chunk(NCHUNK, False, True, False)
            for u in range(LEAD, UNROLL):
                load_slots(0, u)
            with sp.Fori(1, ROUTED // UNROLL) as g:
                for u in range(UNROLL):
                    load_slots(g, u)

        @block.gpsimd
        def _(pool):
            pool.memset(ys[:, :, :].rearrange("p t f -> p (t f)").bitcast(I32), EMPTY).then_inc(sem("fill_ready"), 1)
            pool.memset(base[0:1, 0:2, :], 0.0).then_inc(sem("fill_ready"), 1)
            pool.memset(ones[:, :], 1.0).then_inc(sem("ones_ready"), 1)

            def weight_low(n):
                pool.wait_ge(sem("weights_hi"), 3 * (n + 1))
                js = slice(n * JT // SPLITS, (n + 1) * JT // SPLITS)
                for whole, hi, lo in ((whole_gate, gate_hi, gate_lo), (whole_up, up_hi, up_lo)):
                    nc.gpsimd.tensor_tensor(lo[:, js, :, :].rearrange("p j k o -> p k j o"), whole[:, :, js, :],
                                    hi[:, js, :, :].bitcast(F32).rearrange("p j k o -> p k j o"), ALU.subtract)\
                        .then_inc(sem("weights_lo"), 1)
                nc.gpsimd.tensor_tensor(down_lo[:, js, :], whole_down[:, js, :], down_hi[:, js, :].bitcast(F32),
                                ALU.subtract).then_inc(sem("weights_lo"), 1)

            pool.wait_ge(sem("wo_hi_ready"), 1)
            nc.gpsimd.tensor_tensor(wo_lo[:, :, :], whole_wo, wo_hi[:, :, :].bitcast(F32), ALU.subtract)\
                .then_inc(sem("wo_lo_ready"), 1)
            for n in range(SPLITS):
                weight_low(n)

            def scatter_ids(f):
                wait(pool, "slot_ready", f + 1)
                for t in range(TILES):
                    pool.indirect_dma_start(slot_table[:, :], bass.IndirectOffsetOnAxis(slot[:, t:t + 1], 0),
                                            tokid[:, t:t + 1], None, bounds_check=TABLE - 1, oob_is_err=False)\
                        .then_inc(sem("slots_out"), 16)

            with pool.Fori(0, NCHUNK) as f:
                scatter_ids(f)

            def gather(g, u):
                wait(pool, f"idx_in{u}", 16 * (g + 1))
                pool.indirect_dma_start(gat[:, u, :], None, rows[:, :],
                                        bass.IndirectOffsetOnAxis(idx[:, u:u + 1], 0), bounds_check=TOKENS, oob_is_err=False)\
                    .then_inc(sem(f"gat_in{u}"), 16)

            def gather_first(u):
                pool.indirect_dma_start(gat[:, u, 0:F], None, y_rows[:, :],
                                        bass.IndirectOffsetOnAxis(idx[:, u:u + 1], 0), bounds_check=TOKENS,
                                        oob_is_err=False).then_inc(sem(f"gat_in{u}"), 16)

            def gather_second(u):
                pool.indirect_dma_start(gat[:, u, F:2 * F], None, rows.rearrange("r (h f) -> (r h) f", h=2),
                                        bass.IndirectOffsetOnAxis(idx_half[:, u:u + 1], 0),
                                        bounds_check=2 * TOKENS + 1, oob_is_err=False)\
                    .then_inc(sem(f"late_in{u}"), 16)

            def scatter(g, u):
                wait(pool, "res_ready", g * UNROLL + u + 1)
                pool.indirect_dma_start(out, bass.IndirectOffsetOnAxis(idx[:, u:u + 1], 0),
                                        res[:, u, :], None, bounds_check=TOKENS - 1, oob_is_err=False)\
                    .then_inc(sem(f"res_out{u}"), 16)

            last = ROUTED // UNROLL - 1

            def step(g, u, last_body):
                if not (last_body and u + LEAD >= UNROLL):
                    gather(g + (u + LEAD) // UNROLL, (u + LEAD) % UNROLL)
                scatter(g, u)

            for u in range(LEAD):
                pool.wait_ge(sem(f"idx_in{u}"), 16)
            nc.gpsimd.tensor_scalar(idx_half[:, :], idx[:, 0:LEAD], 2, 1, ALU.mult, ALU.add)\
                .then_inc(sem("halves_ready"), 1)
            pool.wait_ge(sem("halves_ready"), 1)
            pool.wait_ge(sem("filled"), 64)
            pool.wait_ge(sem("ys_out"), 32 * NCHUNK)
            for u in range(LEAD):
                gather_first(u)
            pool.wait_ge(sem("base_out"), 16 * NCHUNK)
            for u in range(LEAD):
                gather_second(u)
            for u in range(UNROLL):
                step(0, u, False)
            with pool.Fori(1, last) as g:
                for u in range(UNROLL):
                    step(g, u, False)
            for u in range(UNROLL):
                step(last, u, True)
            for u in range(UNROLL):
                pool.wait_ge(sem(f"res_out{u}"), 16 * (last + 1))

        @block.tensor
        def _(pe):
            mm = nc.tensor.matmul
            cond = ot[:, :, :].rearrange("p d h -> p (d h)")[:, 0:BATCH]
            affo = sc[:, :, :].rearrange("p a b -> p (a b)")[:, 0:F]
            pe.wait_ge(sem("cond_in"), 48)
            for w in range(2 * KT):
                src = att[:, (w % KT) * P:(w % KT + 1) * P] if w < KT else affo[:, (w % KT) * P:(w % KT + 1) * P]
                last = mm(ps_k[:, w * BATCH:(w + 1) * BATCH], src, cond, start=True, stop=True)
            last.then_inc(sem("style_done"), 1)
            pe.wait_ge(sem("squares_ready"), 2)
            sq = kpad[:, :, :, :].rearrange("p h s d -> p (h s d)")
            w2 = val[:, :, :]
            for k in range(KT):
                last = mm(ps_s[0:BATCH, 0:F], sq[:, k * BATCH:(k + 1) * BATCH], w2[:, 0, k * F:(k + 1) * F],
                          start=(k == 0), stop=(k == KT - 1))
            last.then_inc(sem("sumsq_done"), 1)
            for o in range(KT):
                for k in range(KT):
                    last = mm(ps_o[:, o * BATCH:(o + 1) * BATCH], w2[:, 1, k * F + o * P:k * F + (o + 1) * P],
                              sq[:, (KT + k) * BATCH:(KT + k + 1) * BATCH], start=(k == 0), stop=(k == KT - 1))
            last.then_inc(sem("sumsq_done"), 1)

            pe.wait_ge(sem("demod_k"), 1)
            dk = sc[0:BATCH, :, :].rearrange("p a b -> p (a b)")
            for b in range(CB):
                last = mm(ps_t[:, b * F:(b + 1) * F], ident[0:BATCH, b:b + 1].to_broadcast([BATCH, P]),
                          dk[:, F:2 * F], start=(b == 0), stop=(b == CB - 1), skip_group_check=True)
            last.then_inc(sem("demod_spread"), 1)

            def project(it, t):
                if t == 0:
                    wait(pe, "wkb_ready", it + 1)
                    wait(pe, "xt_in", 16 * (it + 1))
                    wait(pe, "base_ready", 2 * (it - 1) - 1)
                for k in range(KT):
                    last = mm(ps_k[:, 0:F], xt[:, k, t * P:(t + 1) * P], wkb[:, t // (TILES // CB), k, :],
                              start=(k == 0), stop=(k == KT - 1))
                last.then_inc(sem("proj_done"), 1)

            def gram(it, t, ffn_on):
                wait(pe, "keysum_ready", TILES * it + t + 1)
                wait(pe, "s_taken", TILES * it + t)
                if t == 0 and ffn_on:
                    wait(pe, "ys_ready", TILES * it)
                pe.sem_inc(sem("products_passed"), 1)
                for pr in range(PAIRS):
                    for q in range(Q):
                        last = mm(ps_s[32 * q:32 * q + HEADS, 32 * pr:32 * pr + 32],
                                  keysum[32 * q:32 * q + 32, HEADS * pr:HEADS * (pr + 1)],
                                  keyT[32 * q:32 * q + 32, 32 * pr:32 * pr + 32],
                                  start=True, stop=True, tile_position=(32 * q, 32 * q), skip_group_check=True)
                last.then_inc(sem("gram_done"), 1)

            def attend(it, t):
                pe.wait_ge(sem("banks_set"), 2)
                wait(pe, "probT_ready", TILES * it + t + 1)
                wait(pe, "o_taken", TILES * it + t)
                for pr in range(PAIRS):
                    for q in range(Q):
                        last = mm(ps_o[32 * q:32 * q + HEADS, 32 * pr:32 * pr + 32],
                                  probT[32 * q:32 * q + 32, t % 2, 32 * pr:32 * pr + HEADS],
                                  val[32 * q:32 * q + 32, t % 2, 32 * pr:32 * pr + 32],
                                  start=True, stop=True, tile_position=(32 * q, 32 * q), skip_group_check=True)
                last.then_inc(sem("av_done"), 1)

            def turn(it, t):
                wait(pe, "att_ready", TILES * it + t + 1)
                if t == 0:
                    wait(pe, "ys_ready", TILES * it)
                    wait(pe, "rank_taken", it)
                wait(pe, "aT_lo_ready", TILES * it + t)
                for k in range(KT):
                    last = nc.tensor.transpose(ps_t[:, k * P:(k + 1) * P], att[:, k * P:(k + 1) * P], ident)
                last.then_inc(sem("turn_done"), 1)

            def out_linear(it):
                wait(pe, "aT_lo_ready", TILES * (it + 1))
                for o in range(KT):
                    bk = (ps_k, ps_t)[o]
                    cols = slice(o * P, (o + 1) * P)
                    for k in range(KT):
                        mm(bk[:, :], wo_hi[:, k, cols], aT_hi[:, k, :], start=(k == 0), stop=False)
                        mm(bk[:, :], wo_hi[:, k, cols], aT_lo[:, k, :], start=False, stop=False)
                        last = mm(bk[:, :], wo_lo[:, k, cols], aT_hi[:, k, :], start=False, stop=(k == KT - 1))
                    last.then_inc(sem("y_done"), 1)

            def product(bk, hi, lo, j, f):
                for k in range(KT):
                    if j == 0 and f is not None:
                        wait(pe, "y_lo_ready", KT * f + k + 1)
                    mm(bk[:, :], hi[:, j, k, :], y_hi[:, k, :], start=(k == 0), stop=False)
                    mm(bk[:, :], hi[:, j, k, :], y_lo[:, k, :], start=False, stop=False)
                    last = mm(bk[:, :], lo[:, j, k, :], y_hi[:, k, :], start=False, stop=(k == KT - 1))
                return last

            def shared_gate(f, j):
                if j == 0:
                    wait(pe, "y_hi_ready", KT * (f + 1))
                wait(pe, "silu_ready", JT * f + j)
                product(ps_gate, gate_hi, gate_lo, j, f).then_inc(sem("gate_done"), 1)

            def shared_up(f, j):
                wait(pe, "hid_ready", JT * f + j)
                product(ps_up, up_hi, up_lo, j, None).then_inc(sem("up_done"), 1)

            def shared_out(f, j):
                wait(pe, "hid_lo_ready", JT * f + j + 1)
                if j == 0:
                    wait(pe, "base_ready", 2 * f)
                    wait(pe, "ys_ready", TILES * (f + 1))
                for o, bk in ((1, ps_sh1), (0, ps_sh0)):
                    cols = slice(o * P, (o + 1) * P)
                    mm(bk[:, :], down_hi[:, j, cols], hid_hi[:, :], start=(j == 0), stop=False)
                    mm(bk[:, :], down_hi[:, j, cols], hid_lo[:, :], start=False, stop=False)
                    last = mm(bk[:, :], down_lo[:, j, cols], hid_hi[:, :], start=False, stop=(j == JT - 1))
                last.then_inc(sem("down_done"), 1)

            def turn_rows(f):
                wait(pe, "sharedT_ready", KT * (f + 1))
                for n, bk in summed:
                    for t in (2 * n, 2 * n + 1):
                        for o in range(KT):
                            last = nc.tensor.transpose(bk[:, (t % 2) * F + o * P:(t % 2) * F + (o + 1) * P],
                                                       sharedT[:, o, t * P:(t + 1) * P], ident)
                    last.then_inc(sem("rows_turned"), 1)

            def route_in(f):
                wait(pe, "yT_ready", KT * CB * (f + 1))
                wait(pe, "s_taken", TILES * (f + 1))
                wait(pe, "o_taken", TILES * (f + 1))
                for t in range(TILES):
                    if t == TILES - 1:
                        wait(pe, "sharedT_ready", KT * f - 1)
                    for k in range(KT):
                        last = mm(row_banks[t][:, k * P:(k + 1) * P + EXPERTS], yT[:, k, t * P:(t + 1) * P],
                                  turner[:, k * HALF:(k + 1) * HALF], start=(k == 0),
                                  stop=(k == KT - 1), skip_group_check=True)
                    last.then_inc(sem("yrow_done"), 1)

            def route_rank(f):
                wait(pe, "onehot_ready", f + 1)
                wait(pe, "ys_ready", TILES * f + 3)
                width = TILES * EXPERTS
                oh = onehot[:, :, :].rearrange("p t e -> p (t e)")
                at = 2 * HALF
                mm(ps_t[:, at:at + width], tri[:, :], oh, start=True, stop=False, skip_group_check=True)
                for t in range(TILES - 1):
                    lo = (t + 1) * EXPERTS
                    mm(ps_t[:, at + lo:at + width], ones[:, :], oh[:, 0:width - lo], start=False, stop=False,
                       skip_group_check=True)
                for t in range(TILES):
                    last = mm(ps_t[:, at + width:at + width + EXPERTS], ones[:, :], oh[:, t * EXPERTS:(t + 1) * EXPERTS],
                              start=False, stop=(t == TILES - 1), skip_group_check=True)
                last.then_inc(sem("rank_done"), 1)

            def narrow_products(it, j, ffn_on):
                if 1 <= j <= TILES:
                    gram(it, j - 1, ffn_on)
                if 1 <= j < TILES:
                    project(it, j)

            def chunk(it, att_on, ffn_on, first_ffn=False):
                f = it - 1
                for j in range(JT):
                    if ffn_on:
                        if j == 0:
                            route_in(f)
                            if not first_ffn:
                                turn_rows(f - 1)
                        shared_gate(f, j)
                    if att_on and j > UP_FIRST:
                        narrow_products(it, j, ffn_on)
                    if ffn_on:
                        shared_up(f, j)
                    if att_on and j <= UP_FIRST:
                        narrow_products(it, j, ffn_on)
                    if ffn_on:
                        if j == 1:
                            route_rank(f)
                        if j >= 1:
                            shared_out(f, j - 1)
                    if att_on:
                        if j == 0:
                            project(it, j)
                        if 2 <= j <= TILES + 1:
                            attend(it, j - 2)
                        if 3 <= j <= TILES + 2:
                            turn(it, j - 3)
                if att_on:
                    out_linear(it)
                if ffn_on:
                    shared_out(f, JT - 1)

            pe.wait_ge(sem("banks_set"), 2)
            pe.wait_ge(sem("wo_lo_ready"), 1)
            chunk(0, True, False)
            pe.wait_ge(sem("shared_in"), 96)
            pe.wait_ge(sem("weights_hi"), 3 * SPLITS)
            pe.wait_ge(sem("weights_lo"), 3 * SPLITS)
            chunk(1, True, True, True)
            with pe.Fori(2, NCHUNK) as it:
                chunk(it, True, True)
            chunk(NCHUNK, False, True)

            pe.wait_ge(sem("ys_ready"), TILES * NCHUNK)
            pe.wait_ge(sem("gat_in0"), 16)
            for k in range(KT):
                last = nc.tensor.transpose(bank[0][:, k * P:(k + 1) * P], gat[:, 0, k * P:(k + 1) * P], ident)
            last.then_inc(sem("rx_done"), 1)
            turn_rows(NCHUNK - 1)
            pe.wait_ge(sem("expert_in"), EXPERTS_IN)
            pe.wait_ge(sem("list_ready"), 2)
            dn_flat = e_down[:, :, :, :].rearrange("p e k f -> p (e k f)")

            def routed(g, u, first_body, last_body):
                i = UNROLL * g + u
                if not (last_body and u == UNROLL - 1):
                    n = u + 1
                    wait(pe, f"gat_in{n % UNROLL}", 16 * (g + 1 + n // UNROLL))
                    wait(pe, "rx_lo_ready", i)
                    for k in range(KT):
                        last = nc.tensor.transpose(bank[n % 2][:, k * P:(k + 1) * P],
                                                   gat[:, n % UNROLL, k * P:(k + 1) * P], ident)
                    last.then_inc(sem("rx_done"), 1)
                if first_body and u == 1:
                    pe.wait_ge(sem("base_ready"), 2 * NCHUNK)
                wait(pe, "rx_lo_ready", i + 1)
                wait(pe, "gu_lo_ready", i + 1)
                wait(pe, "rhid_ready", i - 1)
                for k in range(KT):
                    xk, wk_ = slice(k * P, (k + 1) * P), slice(k * 2 * EF, (k + 1) * 2 * EF)
                    for n, (xs, ws) in enumerate(((rx_hi, gu_hi), (rx_hi, gu_lo), (rx_lo, gu_hi))):
                        last = mm(bank[3 - u % 2][:, :], xs[:, u % 2, xk], ws[:, u % 2, wk_],
                                  start=(k == 0 and n == 0), stop=(k == KT - 1 and n == 2))
                last.then_inc(sem("rgu_done"), 1)
                if not (first_body and u < 2):
                    routed_down(i - 2, u)
                if not (first_body and u < 1):
                    routed_turn(i - 1, u - 1)

            def routed_down(i, u):
                at = pe.value_load(woff[0:1, bass.ds(i, 1)], min_val=0, max_val=(EXPERTS - 1) * KT * F)
                wait(pe, "rhT_ready", i + 1)
                wait(pe, "res_ready", i - 1)
                for k in range(KT):
                    last = mm(bank[4 + u % 2][:, 0:F], rhT[:, u % 2, k * P:(k + 1) * P],
                              dn_flat[:, bass.ds(at + k * F, F)], start=(k == 0), stop=(k == KT - 1))
                last.then_inc(sem("rdown_done"), 1)

            def routed_turn(i, u):
                wait(pe, "rhid_ready", i + 1)
                wait(pe, "rhT_ready", i - 1)
                for k in range(KT):
                    last = nc.tensor.transpose(bank[6 + u % 2][:, k * P:(k + 1) * P],
                                               rhid[:, u % 2, k * P:(k + 1) * P], ident)
                last.then_inc(sem("rh_done"), 1)

            for u in range(UNROLL):
                routed(0, u, True, False)
            with pe.Fori(1, ROUTED // UNROLL - 1) as g:
                for u in range(UNROLL):
                    routed(g, u, False, False)
            for u in range(UNROLL):
                routed(ROUTED // UNROLL - 1, u, False, True)
            routed_down(ROUTED - 2, 0)
            routed_turn(ROUTED - 1, 1)
            routed_down(ROUTED - 1, 1)

        @block.scalar
        def _(act):
            dk = sc[0:BATCH, :, :].rearrange("p a b -> p (a b)")
            act.wait_ge(sem("sumsq_eps"), 1)
            nc.scalar.activation(dk[:, F:2 * F], dk[:, 0:F], ACT.Sqrt).then_inc(sem("sqrt_k"), 1)
            act.wait_ge(sem("sumsq_eps"), 2)
            nc.scalar.activation(osum[:, 1, :], osum[:, 0, :], ACT.Sqrt).then_inc(sem("sqrt_o"), 1)

            def aT_copy(it, t):
                wait(act, "turn_done", TILES * it + t + 1)
                if t == 0:
                    wait(act, "y_done", KT * it)
                    wait(act, "mod_ready", it + 1)
                for k in range(KT):
                    ins = nc.scalar.activation(aT_hi[:, k, t * P:(t + 1) * P], ps_t[:, k * P:(k + 1) * P], ACT.Copy,
                                               scale=mod[:, KT + k, t // (TILES // CB):t // (TILES // CB) + 1])
                ins.then_inc(sem("aT_ready"), 1)

            def exps(it, t):
                wait(act, "s_taken", TILES * it + t + 1)
                nc.scalar.activation(sc[:, :, :], sc[:, :, :], ACT.Exp, scale=SCALE).then_inc(sem("exp_ready"), 1)

            def yT_copy(it):
                for o in range(KT):
                    wait(act, "y_done", KT * it + o + 1)
                    if o == 0:
                        wait(act, "up_done", JT * it)
                    for b in range(CB):
                        bk = (ps_k, ps_t)[o]
                        nc.scalar.activation(yT[:, o, b * SEQ:(b + 1) * SEQ], bk[:, b * SEQ:(b + 1) * SEQ],
                                             ACT.Identity, bias=biases[:, 2 * KT + o:2 * KT + o + 1],
                                             scale=mod[:, 2 * KT + o, b:b + 1]).then_inc(sem("yT_ready"), 1)
                for o in range(KT):
                    wait(act, "yT_ready", KT * CB * it + CB * (o + 1))
                    nc.scalar.activation(y_hi[:, o, :], yT[:, o, :], ACT.Copy).then_inc(sem("y_hi_ready"), 1)

            def weight_high():
                act.wait_ge(sem("wk_in"), 32)
                nc.scalar.activation(wo_hi[:, :, :], whole_wo, ACT.Copy).then_inc(sem("wo_hi_ready"), 1)
                act.wait_ge(sem("shared_in"), 96)
                for n in range(SPLITS):
                    js = slice(n * JT // SPLITS, (n + 1) * JT // SPLITS)
                    for whole, hi in ((whole_gate, gate_hi), (whole_up, up_hi)):
                        nc.scalar.activation(hi[:, js, :, :].rearrange("p j k o -> p k j o"), whole[:, :, js, :],
                                             ACT.Copy)\
                            .then_inc(sem("weights_hi"), 1)
                    nc.scalar.activation(down_hi[:, js, :], whole_down[:, js, :], ACT.Copy)\
                        .then_inc(sem("weights_hi"), 1)

            def silus(f, j):
                wait(act, "gate_done", JT * f + j + 1)
                wait(act, "hid_ready", JT * f + j)
                nc.scalar.activation(silu[:, :], ps_gate[:, :], ACT.Silu).then_inc(sem("silu_ready"), 1)

            def hid_high(f, j):
                wait(act, "hid_ready", JT * f + j + 1)
                wait(act, "down_done", JT * f + j)
                nc.scalar.activation(hid_hi[:, :], hid[:, :], ACT.Copy).then_inc(sem("hid_hi_ready"), 1)

            def sharedT_copy(f):
                wait(act, "down_done", JT * (f + 1))
                wait(act, "ys_out", 32 * (f + 1))
                for o, bk in ((1, ps_sh1), (0, ps_sh0)):
                    nc.scalar.activation(sharedT[:, o, :], bk[:, :], ACT.Copy).then_inc(sem("sharedT_ready"), 1)

            def score_exp(f):
                wait(act, "top_ready", f + 1)
                nc.scalar.activation(expt[:, :], top[:, :], ACT.Exp, scale=-1.0).then_inc(sem("expt_ready"), 1)

            def ys_copy(f):
                wait(act, "score_ready", f + 1)
                wait(act, "rows_turned", 2 * f)
                for t in range(TILES):
                    wait(act, "yrow_done", TILES * f + t + 1)
                    nc.scalar.activation(ys[:, t, :].rearrange("p (k f) -> p k f", k=KT),
                                         row_banks[t][:, 0:2 * HALF].rearrange("p (k c) -> p k c", k=KT)[:, :, 0:P],
                                         ACT.Copy, scale=score[:, t:t + 1]).then_inc(sem("ys_ready"), 1)

            def chunk(it, att_on, ffn_on):
                f = it - 1
                for j in range(JT):
                    if ffn_on:
                        if j == 0:
                            score_exp(f)
                        silus(f, j)
                        if j == 0:
                            ys_copy(f)
                    if att_on and 1 <= j <= TILES:
                        exps(it, j - 1)
                    if ffn_on:
                        hid_high(f, j)
                    if att_on and 3 <= j <= TILES + 2:
                        aT_copy(it, j - 3)
                if att_on:
                    yT_copy(it)
                if ffn_on and att_on:
                    sharedT_copy(f)

            weight_high()
            chunk(0, True, False)
            act.wait_ge(sem("filled"), 64)
            chunk(1, True, True)
            with act.Fori(2, NCHUNK) as it:
                chunk(it, True, True)
            chunk(NCHUNK, False, True)

            def gu_high(i, u, weights):
                wait(act, "rgu_done", i - 1)
                act.sem_inc(sem("weights_passed"), 1)
                nc.scalar.activation(gu_hi[:, u % 2, :], weights, ACT.Copy).then_inc(sem("gu_hi_ready"), 1)

            def rx_high(i, u):
                wait(act, "rx_done", i + 1)
                wait(act, "rgu_done", i - 1)
                nc.scalar.activation(rx_hi[:, u % 2, :], bank[u % 2][:, 0:KT * P], ACT.Copy)\
                    .then_inc(sem("rx_hi_ready"), 1)

            def routed(g, u, first_body, last_body):
                i = UNROLL * g + u
                if not (last_body and u == UNROLL - 1):
                    rx_high(i + 1, u + 1)
                ahead = not (last_body and u >= UNROLL - 2)
                if ahead:
                    weights = gate_up_of(act, i + 2)
                wait(act, "rgu_done", i + 1)
                wait(act, "rhid_ready", i - 1)
                nc.scalar.activation(rsilu[:, u % 2, :], bank[3 - u % 2][:, 0:EF], ACT.Silu)\
                    .then_inc(sem("rsilu_ready"), 1)
                if ahead:
                    gu_high(i + 2, u + 2, weights)
                if not (first_body and u < 1):
                    rhT_copy(i - 1, u - 1)

            def rhT_copy(i, u):
                wait(act, "rh_done", i + 1)
                wait(act, "rdown_done", i - 1)
                nc.scalar.activation(rhT[:, u % 2, :], bank[6 + u % 2][:, 0:KT * P], ACT.Copy)\
                    .then_inc(sem("rhT_ready"), 1)

            act.wait_ge(sem("list_ready"), 2)
            act.wait_ge(sem("expert_in"), EXPERTS_IN)
            gu_high(0, 0, gate_up_of(act, 0))
            sharedT_copy(NCHUNK - 1)
            rx_high(0, 0)
            gu_high(1, 1, gate_up_of(act, 1))
            for u in range(UNROLL):
                routed(0, u, True, False)
            with act.Fori(1, ROUTED // UNROLL - 1) as g:
                for u in range(UNROLL):
                    routed(g, u, False, False)
            for u in range(UNROLL):
                routed(ROUTED // UNROLL - 1, u, False, True)
            rhT_copy(ROUTED - 1, 1)

        @block.vector
        def _(dve):
            v = nc.vector
            dve.wait_ge(sem("consts_in"), 16)
            v.tensor_copy(tri[:, :], cst[:, C_TRI:C_TRI + P]).then_inc(sem("tri_ready"), 1)
            v.tensor_copy(count[:, :], cst[:, C_BASE:C_BASE + EXPERTS]).then_inc(sem("count_ready"), 1)
            v.tensor_copy(tokid[:, :], cst[:, C_TOK:C_TOK + TILES]).then_inc(sem("tokid_ready"), 1)
            dve.wait_ge(sem("style_done"), 1)
            dve.wait_ge(sem("bias_in"), 32)
            for w in range(2 * KT):
                v.tensor_scalar(mods[:, :, w, :], ps_k[:, w * BATCH:(w + 1) * BATCH]
                                .rearrange("p (c b) -> p c b", b=CB), biases[:, w:w + 1], None, ALU.add)\
                    .then_inc(sem("styles_ready"), 1)
            dve.wait_ge(sem("styles_ready"), 2 * KT)
            sq = kpad[:, :, :, :].rearrange("p h s d -> p (h s d)")[:, 0:2 * KT * BATCH]\
                .rearrange("p (w c b) -> p w c b", w=2 * KT, b=CB)
            for w in range(2 * KT):
                v.tensor_tensor(sq[:, w], mods[:, :, w, :], mods[:, :, w, :], ALU.mult)\
                    .then_inc(sem("sq_part"), 1)
            dve.wait_ge(sem("wk_in"), 32)
            dve.wait_ge(sem("sq_part"), 2 * KT)
            for n, wt in enumerate((wk[:, :, :], whole_wo)):
                flat = wt.rearrange("p k o -> p (k o)")
                v.tensor_tensor(val[:, n, :], flat, flat, ALU.mult).then_inc(sem("squares_ready"), 1)
            dk = sc[0:BATCH, :, :].rearrange("p a b -> p (a b)")
            tmp = probT[0:BATCH, 0, :]
            do_, so_ = osum[:, 0, :], osum[:, 1, :]
            dve.wait_ge(sem("sumsq_done"), 1)
            v.tensor_scalar(dk[:, 0:F], ps_s[0:BATCH, 0:F], EPS, None, ALU.add).then_inc(sem("sumsq_eps"), 1)
            dve.wait_ge(sem("sumsq_done"), 2)
            v.tensor_scalar(do_, ps_o[:, 0:KT * BATCH], EPS, None, ALU.add).then_inc(sem("sumsq_eps"), 1)

            def newton(name, ready, total, root, t, dest):
                dve.wait_ge(sem(ready), 1)
                w_ = t.shape[-1] // 2
                a, b = t[:, 0:w_], t[:, w_:2 * w_]
                v.reciprocal(a, root).then_inc(sem(name), 1)
                dve.wait_ge(sem(name), 1)
                v.tensor_tensor(b, a, a, ALU.mult).then_inc(sem(name), 1)
                dve.wait_ge(sem(name), 2)
                v.tensor_tensor(b, b, total, ALU.mult).then_inc(sem(name), 1)
                dve.wait_ge(sem(name), 3)
                v.tensor_scalar(b, b, -0.5, 1.5, ALU.mult, ALU.add).then_inc(sem(name), 1)
                dve.wait_ge(sem(name), 4)
                return v.tensor_tensor(dest, a if len(dest.shape) == 2 else a.rearrange("p (c b) -> p c b", b=CB),
                                       b if len(dest.shape) == 2 else b.rearrange("p (c b) -> p c b", b=CB), ALU.mult)

            newton("newton_k", "sqrt_k", dk[:, 0:F], dk[:, F:2 * F], tmp, dk[:, F:2 * F]).then_inc(sem("demod_k"), 1)
            for o in range(KT):
                cols = slice(o * BATCH, (o + 1) * BATCH)
                newton(f"newton_o{o}", "sqrt_o", do_[:, cols], so_[:, cols],
                       probT[:, 1, 2 * o * BATCH:2 * (o + 1) * BATCH], mods[:, :, 2 * KT + o, :])\
                    .then_inc(sem("mods_ready"), 1)
            for s in range(2):
                v.tensor_scalar(bias_kp[:, s, :], bias_k[:, :], parity[:, s:s + 1], None, ALU.mult)\
                    .then_inc(sem("bias_ready"), 1)
            dve.wait_ge(sem("bias_ready"), 2)
            dve.wait_ge(sem("mods_ready"), KT)
            dve.wait_ge(sem("ones_ready"), 1)
            dve.wait_ge(sem("demod_out"), 16)

            def modulate(it, first_chunk=False):
                wait(dve, "yT_ready", KT * CB * it)
                wait(dve, "wkb_ready", it)
                wait(dve, "aT_lo_ready", TILES * it)
                v.tensor_copy(mod[:, :, :], mods[:, bass.ds(it, 1), :, :].rearrange("p c w b -> p (c w) b"))\
                    .then_inc(sem("mod_ready"), 1)
                wait(dve, "mod_ready", it + 1)
                if first_chunk:
                    dve.wait_ge(sem("demod_spread"), 1)
                wait(dve, "demod_in", 16 * it)
                wait(dve, "proj_done", TILES * it)
                spread = ps_t[:, :].rearrange("p (b f) -> p b f", b=CB) if first_chunk else demod_b
                for b in range(CB):
                    for k in range(KT):
                        ins = v.scalar_tensor_tensor(wkb[:, b, k, :], wk[:, k, :], mod[:, k, b:b + 1],
                                                     spread[:, b, :], ALU.mult, ALU.mult)
                ins.then_inc(sem("wkb_ready"), 1)

            def keys(it, t):
                wait(dve, "proj_done", TILES * it + t + 1)
                wait(dve, "keyT_ready", TILES * it + t)
                for s in range(2):
                    v.scalar_tensor_tensor(kpad[:, :, s, :], ps_k[:, 0:F].rearrange("p (h d) -> p h d", h=HEADS),
                                           parity[:, s:s + 1],
                                           bias_kp[:, s, :].rearrange("p (h d) -> p h d", h=HEADS),
                                           ALU.mult, ALU.add).then_inc(sem("k_taken"), 1)
                wait(dve, "k_taken", 2 * (TILES * it + t + 1))
                wait(dve, "gram_done", TILES * it + t)
                wait(dve, "val_ready", TILES * it + t)
                v.transpose(keyT[:, :].rearrange("p (t h) -> p h t", h=HEADS),
                            kpad[:, :, :, :].rearrange("p h s d -> p h (s d)")).then_inc(sem("keyT_ready"), 1)
                wait(dve, "keyT_ready", TILES * it + t + 1)
                pairs = keyT[:, :].rearrange("p (r s h) -> p r s h", s=2, h=HEADS)
                v.tensor_tensor(keysum[:, :].rearrange("p (r h) -> p r h", h=HEADS), pairs[:, :, 0, :],
                                pairs[:, :, 1, :], ALU.add).then_inc(sem("keysum_ready"), 1)

            def values(it, t):
                wait(dve, "keyT_ready", TILES * it + t + 1)
                wait(dve, "av_done", TILES * it + t - 1)
                v.transpose(val[:, t % 2, :], keyT[:, :]).then_inc(sem("val_ready"), 1)

            def soft(it, t):
                wait(dve, "gram_done", TILES * it + t + 1)
                wait(dve, "s_taken", TILES * it + t)
                scores = ps_s[:, :].rearrange("p (a b) -> p a b", b=HEADS)
                v.tensor_reduce(rowmax[:, :], scores, AX.X, ALU.max).then_inc(sem("max_ready"), 1)
                wait(dve, "max_ready", TILES * it + t + 1)
                wait(dve, "probT_ready", TILES * it + t)
                v.tensor_tensor(sc[:, :, :], scores, rowmax[:, :].unsqueeze(2).to_broadcast([P, 32, HEADS]),
                                ALU.subtract).then_inc(sem("s_taken"), 1)

            def soft_turn(it, t):
                wait(dve, "exp_ready", TILES * it + t + 1)
                wait(dve, "av_done", TILES * it + t - 1)
                v.transpose(probT[:, t % 2, :], sc[:, :, :].rearrange("p a b -> p (a b)"))\
                    .then_inc(sem("probT_ready"), 1)
                v.tensor_reduce(z[:, :], sc[:, :, :], AX.X, ALU.add).then_inc(sem("z_ready"), 1)
                wait(dve, "z_ready", TILES * it + t + 1)
                v.transpose(zT[:, :], z[:, :]).then_inc(sem("zT_ready"), 1)
                wait(dve, "zT_ready", TILES * it + t + 1)
                v.reciprocal(rz[:, t % 2, :], zT[:, 0:HEADS]).then_inc(sem("rz_ready"), 1)

            def normalise(it, t):
                wait(dve, "av_done", TILES * it + t + 1)
                wait(dve, "att_ready", TILES * it + t)
                v.transpose(ot[:, :, :], ps_o[:, :].rearrange("p (t d) -> p d t", d=D)).then_inc(sem("o_taken"), 1)
                wait(dve, "o_taken", TILES * it + t + 1)
                wait(dve, "rz_ready", TILES * it + t + 1)
                wait(dve, "turn_done", TILES * it + t)
                v.tensor_tensor(att[:, :].rearrange("p (h d) -> p h d", h=HEADS),
                                ot[:, :, 0:HEADS].rearrange("p d h -> p h d"),
                                rz[:, t % 2, :].unsqueeze(2).to_broadcast([P, HEADS, D]), ALU.mult)\
                    .then_inc(sem("att_ready"), 1)

            def att_low(it, t):
                wait(dve, "aT_ready", TILES * it + t + 1)
                if t == 0:
                    wait(dve, "y_done", KT * it)
                for k in range(KT):
                    cols = slice(t * P, (t + 1) * P)
                    ins = v.scalar_tensor_tensor(aT_lo[:, k, cols], ps_t[:, k * P:(k + 1) * P],
                                                 mod[:, KT + k, t // (TILES // CB):t // (TILES // CB) + 1],
                                                 aT_hi[:, k, cols].bitcast(F32), ALU.mult, ALU.subtract)
                ins.then_inc(sem("aT_lo_ready"), 1)

            def split_y(f):
                for o in range(KT):
                    wait(dve, "y_hi_ready", KT * f + o + 1)
                    v.tensor_tensor(y_lo[:, o, :], yT[:, o, :], y_hi[:, o, :].bitcast(F32), ALU.subtract)\
                        .then_inc(sem("y_lo_ready"), 1)

            def hidden(f, j):
                wait(dve, "up_done", JT * f + j + 1)
                wait(dve, "silu_ready", JT * f + j + 1)
                wait(dve, "hid_hi_ready", JT * f + j)
                wait(dve, "hid_lo_ready", JT * f + j)
                v.tensor_tensor(hid[:, :], ps_up[:, :], silu[:, :], ALU.mult).then_inc(sem("hid_ready"), 1)

            def hid_low(f, j):
                wait(dve, "hid_hi_ready", JT * f + j + 1)
                wait(dve, "down_done", JT * f + j)
                v.tensor_tensor(hid_lo[:, :], hid[:, :], hid_hi[:, :].bitcast(F32), ALU.subtract)\
                    .then_inc(sem("hid_lo_ready"), 1)

            def per_tile(a):
                return a.unsqueeze(2).to_broadcast([P, TILES, EXPERTS])

            def per_expert(a):
                return a.unsqueeze(1).to_broadcast([P, TILES, EXPERTS])

            def choose(f):
                logits = [bk[:, P:HALF] for bk in row_banks]
                wait(dve, "score_ready", f)
                wait(dve, "slot_ready", f)
                for t in range(TILES):
                    wait(dve, "yrow_done", TILES * f + t + 1)
                    ins = v.tensor_reduce(top[:, t:t + 1], logits[t], AX.X, ALU.max)
                ins.then_inc(sem("top_ready"), 1)
                wait(dve, "top_ready", f + 1)
                for t in range(TILES):
                    ins = v.tensor_scalar(eq[:, t, :], logits[t], top[:, t:t + 1], None, ALU.is_equal)
                ins.then_inc(sem("eq_ready"), 1)
                wait(dve, "eq_ready", f + 1)
                v.tensor_tensor(pick[:, :, :], eq[:, :, :], per_expert(erev), ALU.mult).then_inc(sem("pick_ready"), 1)
                wait(dve, "pick_ready", f + 1)
                v.tensor_reduce(pickmax[:, :], pick[:, :, :], AX.X, ALU.max).then_inc(sem("pickmax_ready"), 1)
                wait(dve, "pickmax_ready", f + 1)
                v.tensor_tensor(onehot[:, :, :], pick[:, :, :], per_tile(pickmax[:, :]), ALU.is_equal)\
                    .then_inc(sem("onehot_ready"), 1)

            def score_of(f):
                wait(dve, "expt_ready", f + 1)
                wait(dve, "ys_ready", TILES * f)
                v.tensor_scalar(ex1[:, :], expt[:, :], 1.0, None, ALU.add).then_inc(sem("ex1_ready"), 1)
                wait(dve, "ex1_ready", f + 1)
                v.reciprocal(score[:, :], ex1[:, :]).then_inc(sem("score_ready"), 1)

            def place(f, first_chunk):
                width, at = TILES * EXPERTS, 2 * HALF
                wait(dve, "rank_done", f + 1)
                wait(dve, "count_ready", f + 1)
                v.tensor_tensor(rank[:, :, :], ps_t[:, at:at + width].rearrange("p (t e) -> p t e", e=EXPERTS),
                                per_expert(count[:, :]), ALU.add).then_inc(sem("rank_ready"), 1)
                wait(dve, "rank_ready", f + 1)
                v.tensor_tensor(count[:, :], count[:, :], ps_t[:, at + width:at + width + EXPERTS], ALU.add)\
                    .then_inc(sem("count_ready"), 1)
                wait(dve, "count_ready", f + 2)
                v.tensor_tensor(slotsel[:, :, :], rank[:, :, :], onehot[:, :, :], ALU.mult)\
                    .then_inc(sem("rank_taken"), 1)
                wait(dve, "rank_taken", f + 1)
                v.tensor_reduce(slotf[:, :], slotsel[:, :, :], AX.X, ALU.add).then_inc(sem("slotf_ready"), 1)
                wait(dve, "slotf_ready", f + 1)
                if not first_chunk:
                    wait(dve, "slots_out", 16 * TILES * f)
                    wait(dve, "tokid_ready", f)
                    v.tensor_scalar(tokid[:, :], tokid[:, :], float(CHUNK), None, ALU.add)\
                        .then_inc(sem("tokid_ready"), 1)
                wait(dve, "tokid_ready", f + 1)
                v.tensor_copy(slot[:, :], slotf[:, :]).then_inc(sem("slot_ready"), 1)

            def sum_rows(f):
                wait(dve, "residual_in", 16 * (f + 1))
                for turned, (n, bk) in enumerate(summed):
                    wait(dve, "rows_turned", 2 * f + turned + 1)
                    v.tensor_tensor(base[:, 2 * n:2 * n + 2, :], bk[:, :].rearrange("p (t f) -> p t f", f=F),
                                    base[:, 2 * n:2 * n + 2, :], ALU.add).then_inc(sem("base_ready"), 1)

            step = [0]

            def link(ins):
                step[0] += 1
                ins.then_inc(sem("list_step"), 1)
                dve.wait_ge(sem("list_step"), step[0])

            numbers = cst[0:1, C_TILE:C_TILE + ROUTED]

            def list_tiles(j):
                if j == 1:
                    dve.wait_ge(sem("count_ready"), NCHUNK + 1)
                    NK = TOKENS // P
                    link(v.tensor_tensor(held[:, :], count[0:1, :], cst[0:1, C_BASE:C_BASE + EXPERTS], ALU.subtract))
                    link(v.tensor_tensor(more[:, :, :], held[:, :].unsqueeze(2).to_broadcast([1, EXPERTS, NK]),
                                         cst[0:1, C_STEP:C_STEP + NK].unsqueeze(1).to_broadcast([1, EXPERTS, NK]),
                                         ALU.is_gt))
                    link(v.tensor_reduce(ntile[:, :], more[:, :, :], AX.X, ALU.add))
                    link(v.memset(held[:, :], 1.0))
                    link(v.tensor_tensor_scan(tend[:, :], held[:, :], ntile[:, :], 0.0, ALU.mult, ALU.add))
                if j == 2:
                    link(v.tensor_tensor(before[:, :, :], tend[:, :].unsqueeze(1).to_broadcast([1, ROUTED, EXPERTS]),
                                         numbers.unsqueeze(2).to_broadcast([1, ROUTED, EXPERTS]), ALU.is_le))
                if j == 3:
                    link(v.tensor_reduce(which[:, :], before[:, :, :], AX.X, ALU.add))
                    link(v.tensor_tensor(weighed[:, :, :], before[:, :, :],
                                         ntile[:, :].unsqueeze(1).to_broadcast([1, ROUTED, EXPERTS]), ALU.mult))
                if j == 4:
                    link(v.tensor_reduce(first[:, :], weighed[:, :, :], AX.X, ALU.add))
                    link(v.tensor_tensor(within[:, :], numbers, first[:, :], ALU.subtract))
                    link(v.tensor_scalar(within[:, :], within[:, :], float(P), None, ALU.mult))
                    link(v.scalar_tensor_tensor(offf[:, :], which[:, :], float(TOKENS), within[:, :], ALU.mult,
                                                ALU.add))
                    v.tensor_copy(off[:, :], offf[:, :]).then_inc(sem("list_ready"), 1)
                    link(v.tensor_scalar(wofff[:, :], which[:, :], float(EXPERTS - 1), float(KT * F), ALU.min,
                                         ALU.mult))
                    v.tensor_copy(woff[:, :], wofff[:, :]).then_inc(sem("list_ready"), 1)

            def chunk(it, att_on, ffn_on, first_ffn=False):
                f = it - 1
                if att_on:
                    modulate(it, not ffn_on)
                if ffn_on:
                    split_y(f)
                    choose(f)
                    if not first_ffn:
                        sum_rows(f - 1)
                    score_of(f)
                for j in range(JT):
                    if ffn_on and j <= UP_FIRST:
                        hidden(f, j)
                    if att_on:
                        if 1 <= j <= TILES:
                            soft(it, j - 1)
                            values(it, j - 1)
                        if j < TILES:
                            keys(it, j)
                    if ffn_on and j > UP_FIRST:
                        hidden(f, j)
                    if att_on and 1 <= j <= TILES:
                        soft_turn(it, j - 1)
                    if ffn_on and j == 1:
                        place(f, first_ffn)
                    if ffn_on:
                        hid_low(f, j)
                    if att_on and 2 <= j <= TILES + 1:
                        normalise(it, j - 2)
                    if att_on and 3 <= j <= TILES + 2:
                        att_low(it, j - 3)
                    if not att_on:
                        list_tiles(j)

            v.memset(ps_s[:, :], 0.0).then_inc(sem("banks_set"), 1)
            v.memset(ps_o[:, :], 0.0).then_inc(sem("banks_set"), 1)
            chunk(0, True, False)
            dve.wait_ge(sem("filled"), 64)
            chunk(1, True, True, True)
            with dve.Fori(2, NCHUNK) as it:
                chunk(it, True, True)
            chunk(NCHUNK, False, True)

            def gu_low(i, u, weights):
                wait(dve, "gu_hi_ready", i + 1)
                v.tensor_tensor(gu_lo[:, u % 2, :], weights, gu_hi[:, u % 2, :].bitcast(F32), ALU.subtract)\
                    .then_inc(sem("gu_lo_ready"), 1)

            def rx_low(i, u):
                wait(dve, "rx_hi_ready", i + 1)
                v.tensor_tensor(rx_lo[:, u % 2, :], bank[u % 2][:, 0:KT * P], rx_hi[:, u % 2, :].bitcast(F32),
                                ALU.subtract).then_inc(sem("rx_lo_ready"), 1)

            def rhidden(g, u, first_body, last_body):
                i = UNROLL * g + u
                if not (last_body and u == UNROLL - 1):
                    rx_low(i + 1, u + 1)
                ahead = not (last_body and u >= UNROLL - 2)
                if ahead:
                    weights = gate_up_of(dve, i + 2)
                wait(dve, "rgu_done", i + 1)
                wait(dve, "rsilu_ready", i + 1)
                wait(dve, "rh_done", i - 1)
                v.tensor_tensor(rhid[:, u % 2, :], bank[3 - u % 2][:, EF:2 * EF], rsilu[:, u % 2, :], ALU.mult)\
                    .then_inc(sem("rhid_ready"), 1)
                if not (first_body and u < 2):
                    result(i - 2, u - 2, g if u >= 2 else g - 1)
                if ahead:
                    gu_low(i + 2, u + 2, weights)

            def result(i, u, g):
                wait(dve, "rdown_done", i + 1)
                if isinstance(i, int) and i < LEAD:
                    dve.wait_ge(sem(f"late_in{u}"), 16)
                wait(dve, f"res_out{u % UNROLL}", 16 * g)
                v.tensor_tensor(res[:, u % UNROLL, :], bank[4 + u % 2][:, 0:F], gat[:, u % UNROLL, F:2 * F], ALU.add)\
                    .then_inc(sem("res_ready"), 1)

            dve.wait_ge(sem("expert_in"), EXPERTS_IN)
            gu_low(0, 0, gate_up_of(dve, 0))
            rx_low(0, 0)
            sum_rows(NCHUNK - 1)
            gu_low(1, 1, gate_up_of(dve, 1))
            for u in range(UNROLL):
                rhidden(0, u, True, False)
            with dve.Fori(1, ROUTED // UNROLL - 1) as g:
                for u in range(UNROLL):
                    rhidden(g, u, False, False)
            for u in range(UNROLL):
                rhidden(ROUTED // UNROLL - 1, u, False, True)
            for u in (UNROLL - 2, UNROLL - 1):
                result(ROUTED - UNROLL + u, u, ROUTED // UNROLL - 1)


NAMES = ["xT", "x", "condT", "k_affT", "k_wT", "k_b", "o_affT", "o_wT", "bias_cols", "routerT",
         "gate_up", "down", "sh_gateT", "sh_upT", "sh_downT", "consts"]


def constants(np):
    c = np.zeros((P, C_END), np.float32)
    i = np.arange(P)
    c[:, C_ID:C_ID + P] = np.eye(P)
    c[:, C_TRI:C_TRI + P] = i[:, None] < i[None, :]
    c[:, C_PAR:C_PAR + 2] = i[:, None] % 2 == np.arange(2)[None, :]
    c[:, C_REV:C_REV + EXPERTS] = EXPERTS - np.arange(EXPERTS)
    c[:, C_BASE:C_BASE + EXPERTS] = TOKENS * np.arange(EXPERTS)
    c[:, C_STEP:C_STEP + TOKENS // P] = P * np.arange(TOKENS // P)
    c[:, C_TILE:C_TILE + ROUTED] = np.arange(ROUTED)
    c[:, C_TOK:C_TOK + TILES] = i[:, None] + P * np.arange(TILES)[None, :]
    return c


def kernel(x, cond_512, L0_cond_k_aff_w, L0_cond_k_aff_b, L0_cond_k_w, L0_cond_k_b, L0_cond_o_aff_w,
           L0_cond_o_aff_b, L0_cond_o_w, L0_cond_o_b, L0_ffn_router_w, L0_ffn_gate_up_proj, L0_ffn_down_proj,
           L0_ffn_shared_gate_w, L0_ffn_shared_up_w, L0_ffn_shared_down_w):
    import numpy as np
    import concourse.bacc as bacc
    from concourse.bass_utils import run_bass_kernel_spmd

    flat = np.ascontiguousarray(x).reshape(TOKENS, F)
    data = dict(
        xT=flat.reshape(NCHUNK, CHUNK, KT, P).transpose(0, 3, 2, 1),
        x=flat.reshape(TOKENS // P, P, F),
        condT=np.asarray(cond_512).T,
        k_affT=np.asarray(L0_cond_k_aff_w).T, k_wT=np.asarray(L0_cond_k_w).T, k_b=L0_cond_k_b,
        o_affT=np.asarray(L0_cond_o_aff_w).T, o_wT=np.asarray(L0_cond_o_w).T,
        bias_cols=np.stack([np.asarray(b).reshape(KT, P).T
                            for b in (L0_cond_k_aff_b, L0_cond_o_aff_b, L0_cond_o_b)], axis=1).reshape(P, 3 * KT),
        routerT=np.asarray(L0_ffn_router_w).T, gate_up=L0_ffn_gate_up_proj, down=L0_ffn_down_proj,
        sh_gateT=np.asarray(L0_ffn_shared_gate_w).T, sh_upT=np.asarray(L0_ffn_shared_up_w).T,
        sh_downT=np.asarray(L0_ffn_shared_down_w).T, consts=constants(np),
    )
    nc = bacc.Bacc("TRN2", target_bir_lowering=False, num_devices=1)
    arrays, args = {}, []
    for name in NAMES:
        a = np.ascontiguousarray(data[name])
        arrays["in_" + name] = a
        args.append(nc.dram_tensor("in_" + name, a.shape, mybir.dt.from_np(a.dtype), kind="ExternalInput").ap())
    out = nc.dram_tensor("out_rows", (TOKENS, F), F32, kind="ExternalOutput").ap()
    build_program(nc, *args, out)
    r = run_bass_kernel_spmd(nc, [arrays], core_ids=[0])
    return r.results[0]["out_rows"].reshape(BATCH, SEQ, F)
```
